# Optimizing a Trainium2 kernel written in Bass

```python
import numpy as np
import jax
import jax.numpy as jnp

def _softmax(x, axis=-1):
    return jax.nn.softmax(x, axis=axis)
def _gelu(x):
    return jax.nn.gelu(x, approximate=True)
def _silu(x):
    return jax.nn.silu(x)
def _sigmoid(x):
    return jax.nn.sigmoid(x)
def _layernorm(x, axis=-1, eps=1e-5):
    m = jnp.mean(x, axis=axis, keepdims=True)
    v = jnp.var(x, axis=axis, keepdims=True)
    return (x - m) / jnp.sqrt(v + eps)
def _scatter_add(tgt, idx, src, axis=0):
    return tgt.at[idx].add(src)
def _segment_sum(src, seg, n):
    return jax.ops.segment_sum(src, seg, n)

kernel_name = 'mk_vit_tower_d1_tok_img512_a37709'

def setup_inputs(seed: int = 0):
    np.random.seed(seed)
    _w = jnp.asarray
    def _rec_inputs():
        import jax
        import jax.numpy as jnp
        _rk = jax.random.key(seed)
        x = (0.000249115 + 0.999088 * jax.random.normal(jax.random.fold_in(_rk, 1), (64, 256, 257, 2), jnp.float32))
        return x
    x = _rec_inputs()
    def _L0_tok_setup():
        import jax, jax.numpy as jnp
        import numpy as np
        NLAT = 256
        NLON = 2 * NLAT
        LMAX = NLAT
        MMAX = NLAT + 1
        ALPHA = 2.0
        TAU = 3.0
        SIGMA = TAU ** (0.5 * (2 * ALPHA - 2.0))
        RADIUS = 1.0

        def _legpoly(mmax, lmax, x):
            nmax = max(mmax, lmax)
            vdm = np.zeros((nmax, nmax, len(x)), dtype=np.float64)
            norm_factor = 1.0 / np.sqrt(4.0 * np.pi)
            vdm[0, 0, :] = norm_factor / np.sqrt(4.0 * np.pi)
            for l in range(1, nmax):
                vdm[l - 1, l] = np.sqrt(2 * l + 1) * x * vdm[l - 1, l - 1]
                vdm[l, l] = np.sqrt((2 * l + 1) * (1 + x) * (1 - x) / (2 * l)) * vdm[l - 1, l - 1]
            for l in range(2, nmax):
                for m in range(0, l - 1):
                    a = np.sqrt((2 * l - 1) / (l - m) * (2 * l + 1) / (l + m))
                    b = np.sqrt((l + m - 1) / (l - m) * (2 * l + 1) / (2 * l - 3) * (l - m - 1) / (l + m))
                    vdm[m, l] = x * a * vdm[m, l - 1] - b * vdm[m, l - 2]
            vdm = vdm[:mmax, :lmax]
            for m in range(1, mmax, 2):
                vdm[m] *= -1.0
            return vdm

        def _make_buffers():
            tj = np.pi * np.arange(NLAT) / (NLAT - 1)
            x = np.flip(np.cos(tj)).copy()
            pct = _legpoly(MMAX, LMAX, x).astype(np.float32)
            l = np.arange(NLAT, dtype=np.float64)
            e = SIGMA * (l * (l + 1) / RADIUS ** 2 + TAU ** 2) ** (-ALPHA / 2.0)
            se = np.tril(np.repeat(e[:, None], NLAT + 1, axis=1))
            se[0, 0] = 0.0
            sqrt_eig = se[None].astype(np.float32)
            return (jnp.asarray(pct), jnp.asarray(sqrt_eig))
        key = jax.random.key(seed)
        xi = jax.random.normal(key, (8, NLAT, NLAT + 1, 2), dtype=jnp.float32)
        pct, sqrt_eig = _make_buffers()
        return {'xi': xi, 'sqrt_eig': sqrt_eig, 'pct': pct, 'N': 8}
    _L0_tok_all = _L0_tok_setup()
    _L0_tok_in = {k: v for k, v in _L0_tok_all.items() if k in ('sqrt_eig', 'pct', )}
    del _L0_tok_all

    def _L0_attn_setup():
        import jax, jax.numpy as jnp
        import numpy as np
        ATTENTION_WIDTH = 12
        key = jax.random.key(seed)
        k1, k2 = jax.random.split(key)
        B, S, D = (8, 2048, 512)
        x = jax.random.normal(k1, (B, S, D), dtype=jnp.float32)
        K = jax.random.normal(k2, (D, D), dtype=jnp.float32) * np.sqrt(2.0 / (D + D)).astype(np.float32)
        temperature = jnp.ones((1,), dtype=jnp.float32)
        bias = jnp.zeros((1,), dtype=jnp.float32)
        return {'x': x, 'K': K, 'temperature': temperature, 'bias': bias}
    _L0_attn_all = _L0_attn_setup()
    _L0_attn_in = {k: v for k, v in _L0_attn_all.items() if k in ('K', 'temperature', 'bias', )}
    del _L0_attn_all

    def _L0_ffn_setup():
        import jax, jax.numpy as jnp
        import numpy as np
        MARK_AX = 0
        OP_MUL = 1
        OPCODE_BASE = 2
        ALU_LO, ALU_HI = (64, 80)
        AX_CARRY_LO, AX_CARRY_HI = (96, 112)
        OUTPUT_LO, OUTPUT_HI = (128, 144)
        NIB_A, NIB_B, RESULT, OP_START = (0, 1, 2, 3)
        GE_DIM = 160
        N_POS = 8
        N_LAYERS = 7
        OPCODE = 27

        def _decode_nibble(x16):
            return jnp.argmax(x16 > 0.5, axis=-1).astype(x16.dtype)
        key = jax.random.key(seed)
        k1, k2, k3 = jax.random.split(key, 3)
        x_bd = jax.random.uniform(k1, (4, 8192, 512), dtype=jnp.float32)
        W = jax.random.normal(k2, (N_LAYERS, GE_DIM, GE_DIM), dtype=jnp.float32) * 0.05
        b = jax.random.normal(k3, (N_LAYERS, GE_DIM), dtype=jnp.float32) * 0.01
        return {'x_bd': x_bd, 'W': W, 'b': b}
    _L0_ffn_all = _L0_ffn_setup()
    _L0_ffn_in = {k: v for k, v in _L0_ffn_all.items() if k in ('W', 'b', )}
    del _L0_ffn_all

    return {
        "x": x,
        "L0_tok_sqrt_eig": _L0_tok_in["sqrt_eig"],
        "L0_tok_pct": _L0_tok_in["pct"],
        "L0_attn_K": _L0_attn_in["K"],
        "L0_attn_temperature": _L0_attn_in["temperature"],
        "L0_attn_bias": _L0_attn_in["bias"],
        "L0_ffn_W": _L0_ffn_in["W"],
        "L0_ffn_b": _L0_ffn_in["b"],
    }

def reference(x, L0_tok_sqrt_eig, L0_tok_pct, L0_attn_K, L0_attn_temperature, L0_attn_bias, L0_ffn_W, L0_ffn_b):
    import jax
    import jax.numpy as jnp
    def _L0_tok_ref(xi, sqrt_eig, pct, N):
        import jax, jax.numpy as jnp
        import numpy as np
        NLAT = 256
        NLON = 2 * NLAT
        LMAX = NLAT
        MMAX = NLAT + 1
        ALPHA = 2.0
        TAU = 3.0
        SIGMA = TAU ** (0.5 * (2 * ALPHA - 2.0))
        RADIUS = 1.0

        def _legpoly(mmax, lmax, x):
            nmax = max(mmax, lmax)
            vdm = np.zeros((nmax, nmax, len(x)), dtype=np.float64)
            norm_factor = 1.0 / np.sqrt(4.0 * np.pi)
            vdm[0, 0, :] = norm_factor / np.sqrt(4.0 * np.pi)
            for l in range(1, nmax):
                vdm[l - 1, l] = np.sqrt(2 * l + 1) * x * vdm[l - 1, l - 1]
                vdm[l, l] = np.sqrt((2 * l + 1) * (1 + x) * (1 - x) / (2 * l)) * vdm[l - 1, l - 1]
            for l in range(2, nmax):
                for m in range(0, l - 1):
                    a = np.sqrt((2 * l - 1) / (l - m) * (2 * l + 1) / (l + m))
                    b = np.sqrt((l + m - 1) / (l - m) * (2 * l + 1) / (2 * l - 3) * (l - m - 1) / (l + m))
                    vdm[m, l] = x * a * vdm[m, l - 1] - b * vdm[m, l - 2]
            vdm = vdm[:mmax, :lmax]
            for m in range(1, mmax, 2):
                vdm[m] *= -1.0
            return vdm

        def _make_buffers():
            tj = np.pi * np.arange(NLAT) / (NLAT - 1)
            x = np.flip(np.cos(tj)).copy()
            pct = _legpoly(MMAX, LMAX, x).astype(np.float32)
            l = np.arange(NLAT, dtype=np.float64)
            e = SIGMA * (l * (l + 1) / RADIUS ** 2 + TAU ** 2) ** (-ALPHA / 2.0)
            se = np.tril(np.repeat(e[:, None], NLAT + 1, axis=1))
            se[0, 0] = 0.0
            sqrt_eig = se[None].astype(np.float32)
            return (jnp.asarray(pct), jnp.asarray(sqrt_eig))
        coeff = jax.lax.complex(xi[..., 0], xi[..., 1]) * sqrt_eig.astype(jnp.complex64)
        x = jnp.einsum('nlm,mlk->nkm', coeff, pct.astype(jnp.complex64))
        u = jnp.fft.irfft(x, n=NLON, axis=-1, norm='forward')
        return u

    def _L0_attn_ref(x, K, temperature, bias):
        import jax, jax.numpy as jnp
        import numpy as np
        ATTENTION_WIDTH = 12
        S = x.shape[1]
        key = jnp.einsum('bsd,de->bse', x, K)
        logits = jnp.tanh(jnp.einsum('bsd,btd->bst', key, x) + bias[0])
        idx = jnp.arange(S)
        lower = idx - ATTENTION_WIDTH // 2
        upper = lower + ATTENTION_WIDTH
        band = (lower[:, None] <= idx[None, :]) & (idx[None, :] < upper[:, None])
        logits = logits - 10000.0 * (1.0 - band.astype(logits.dtype))
        logits = logits * temperature
        scores = jax.nn.softmax(logits, axis=-1)
        return jnp.einsum('bst,btd->bsd', scores, x)

    def _L0_ffn_ref(x_bd, W, b):
        import jax, jax.numpy as jnp
        import numpy as np
        MARK_AX = 0
        OP_MUL = 1
        OPCODE_BASE = 2
        ALU_LO, ALU_HI = (64, 80)
        AX_CARRY_LO, AX_CARRY_HI = (96, 112)
        OUTPUT_LO, OUTPUT_HI = (128, 144)
        NIB_A, NIB_B, RESULT, OP_START = (0, 1, 2, 3)
        GE_DIM = 160
        N_POS = 8
        N_LAYERS = 7
        OPCODE = 27

        def _decode_nibble(x16):
            return jnp.argmax(x16 > 0.5, axis=-1).astype(x16.dtype)
        B, S, D = x_bd.shape
        mask = (x_bd[..., MARK_AX] >= 0.5) & (x_bd[..., OP_MUL] >= 0.5)
        a_lo = _decode_nibble(x_bd[..., ALU_LO:ALU_LO + 16])
        a_hi = _decode_nibble(x_bd[..., ALU_HI:ALU_HI + 16])
        b_lo = _decode_nibble(x_bd[..., AX_CARRY_LO:AX_CARRY_LO + 16])
        b_hi = _decode_nibble(x_bd[..., AX_CARRY_HI:AX_CARRY_HI + 16])
        op_val = x_bd[..., OPCODE_BASE + OPCODE]
        x_ge = jnp.zeros((B, S, N_POS, GE_DIM), dtype=x_bd.dtype)
        x_ge = x_ge.at[..., 0, NIB_A].set(a_lo)
        x_ge = x_ge.at[..., 1, NIB_A].set(a_hi)
        x_ge = x_ge.at[..., 0, NIB_B].set(b_lo)
        x_ge = x_ge.at[..., 1, NIB_B].set(b_hi)
        x_ge = x_ge.at[..., :, OP_START + OPCODE].set(op_val[..., None])
        h = x_ge
        for i in range(N_LAYERS):
            h = jnp.einsum('bspd,ed->bspe', h, W[i]) + b[i]
            if i < N_LAYERS - 1:
                h = jax.nn.relu(h)
        res_lo = jnp.clip(jnp.round(h[..., 0, RESULT]), 0, 15).astype(jnp.int32)
        res_hi = jnp.clip(jnp.round(h[..., 1, RESULT]), 0, 15).astype(jnp.int32)
        m = mask[..., None].astype(x_bd.dtype)
        add_lo = 2.0 * jax.nn.one_hot(res_lo, 16, dtype=x_bd.dtype) * m
        add_hi = 2.0 * jax.nn.one_hot(res_hi, 16, dtype=x_bd.dtype) * m
        out = x_bd.at[..., OUTPUT_LO:OUTPUT_LO + 16].add(add_lo)
        out = out.at[..., OUTPUT_HI:OUTPUT_HI + 16].add(add_hi)
        return out

    h = _L0_tok_ref(x, L0_tok_sqrt_eig, L0_tok_pct, 64)
    h = h + _L0_attn_ref(_layernorm(h, axis=-1), L0_attn_K, L0_attn_temperature, L0_attn_bias)
    h = h + _L0_ffn_ref(_layernorm(h, axis=-1), L0_ffn_W, L0_ffn_b)
    return h


_drawn_inputs = setup_inputs


def setup_inputs(seed=0):
    import zlib

    import numpy as np

    out = dict(_drawn_inputs(seed))
    spreads = {}
    factors = {}
    for name, (base, spread) in spreads.items():
        noise = np.random.default_rng([zlib.crc32(name.encode()), seed]).standard_normal(out[name].shape)
        drawn = base * np.exp(spread * noise) if base else spread * noise
        out[name] = jnp.asarray(drawn.astype(out[name].dtype))
    for name, factor in factors.items():
        out[name] = (out[name] * factor).astype(out[name].dtype)
    return out
```

```python
from contextlib import ExitStack

import numpy as np

import concourse.bass as bass
from concourse import mybir

F32 = mybir.dt.float32
F32R = mybir.dt.float32r
U32 = mybir.dt.uint32
ACT = mybir.ActivationFunctionType
ALU = mybir.AluOpType
AX_X = mybir.AxisListType.X

P = 128
NB, NLAT, MMAX, NLON = 64, 256, 257, 512
TILES = NLAT // P
CH = NLON // P
EPS = 1e-5

GM = 8
GROUPS = (MMAX - 1) // GM
RING1 = 4

ROW = 40
OUT_LO, OUT_W = 128, 32
FAR = 1048576.0
HALF = NLON // 2
MID = 5
WCOLS = 3 * P + 224
TJ = 8
MAGIC = 12582912.0


def wait(eng, sem, value):
    if isinstance(value, int) and value <= 0:
        return
    eng.wait_ge(sem, value)


def stage1_spectrum(nc, ctx0, xs_in, pct_in, se_in, spec, recs):
    with ExitStack() as ctx:
        def sb(name, shape, dt=F32):
            return ctx.enter_context(nc.sbuf_tensor(name, shape, dt))

        def sem(name):
            return ctx.enter_context(nc.semaphore(name))

        xg = sb("xg", [P, RING1, GM * 2, P])
        pg = sb("pg", [P, RING1, GM * 2, NLAT])
        cg = sb("cg", [P, 2, GM * 2, P])
        se = sb("se", [P, MMAX * 2])
        stage = sb("stage", [P, 2, GM, NLAT])
        rec0 = sb("rec0", [P, 32, ROW])
        bank = [ctx.enter_context(nc.psum_tensor(f"s1b{i}", [P, 2, NLAT], F32)) for i in range(8)]

        se_loaded = sem("se_loaded")
        loaded = [sem(f"s1_loaded{i}") for i in range(RING1)]
        scaled = sem("s1_scaled")
        summed = sem("s1_summed")
        copied = sem("s1_copied")
        stored = [sem(f"s1_stored{i}") for i in range(2)]
        rec_filled = sem("rec_filled")
        rec_stored = sem("rec_stored")

        block = ctx.enter_context(nc.Block())

        @block.sync
        def _(sp):
            def load(g, b):
                sp.dma_start(xg[:, b], xs_in[:, bass.ds(g * GM * 2, GM * 2), :]).then_inc(loaded[b], 16)
                sp.dma_start(pg[:, b], pct_in[:, bass.ds(g * GM * 2, GM * 2), :]).then_inc(loaded[b], 16)

            sp.dma_start(se[:, :], se_in).then_inc(se_loaded, 16)
            for b in range(RING1):
                load(b, b)
            with nc.sync.Fori(RING1, GROUPS - RING1 + 1, RING1) as g0:
                for b in range(RING1):
                    sp.wait_ge(summed, g0 + (b - RING1 + 1))
                    load(g0 + b, b)
            sp.wait_ge(summed, GROUPS - RING1 + 1)
            sp.dma_start(xg[:, 0, 0:2], xs_in[:, GROUPS * GM * 2:, :]).then_inc(loaded[0], 16)
            sp.dma_start(pg[:, 0, 0:2], pct_in[:, GROUPS * GM * 2:, :]).then_inc(loaded[0], 16)

        @block.vector
        def _(dve):
            def scale(g, b):
                wait(dve, summed, g - 1)
                nc.vector.tensor_tensor(
                    cg[:, b % 2], xg[:, b], se_view(g), ALU.mult).then_inc(scaled, 1)

            def se_view(g):
                v = se[:, bass.ds(g * GM * 2, GM * 2)]
                return v.unsqueeze(2).to_broadcast([P, GM * 2, P])

            nc.vector.memset(rec0[:, :, 1:ROW], 0.0).then_inc(rec_filled, 1)
            nc.vector.memset(rec0[:, :, 0:1], FAR).then_inc(rec_filled, 1)
            dve.wait_ge(se_loaded, 16)
            for b in range(RING1):
                dve.wait_ge(loaded[b], 32)
                scale(b, b)
            with nc.vector.Fori(RING1, GROUPS - RING1 + 1, RING1) as g0:
                for b in range(RING1):
                    dve.wait_ge(loaded[b], g0 * (32 // RING1) + 32)
                    scale(g0 + b, b)
            dve.wait_ge(loaded[0], 32 * (GROUPS // RING1 + 1))
            dve.wait_ge(summed, GROUPS - 1)
            nc.vector.tensor_tensor(
                cg[:, 0, 0:2], xg[:, 0, 0:2],
                se[:, GROUPS * GM * 2:].unsqueeze(2).to_broadcast([P, 2, P]), ALU.mult).then_inc(scaled, 1)

        @block.tensor
        def _(pe):
            def multiply(g, b):
                pe.wait_ge(scaled, g + 1)
                wait(pe, copied, (g - 1) * 4)
                for m in range(GM):
                    for h in range(2):
                        last = nc.tensor.matmul(bank[(b % 2) * 4 + m // 2][:, m % 2, :],
                                                cg[:, b % 2, m * 2 + h, :], pg[:, b, m * 2 + h, :],
                                                start=(h == 0), stop=(h == 1))
                last.then_inc(summed, 1)

            for b in range(RING1):
                multiply(b, b)
            with nc.tensor.Fori(RING1, GROUPS - RING1 + 1, RING1) as g0:
                for b in range(RING1):
                    multiply(g0 + b, b)
            pe.wait_ge(scaled, GROUPS + 1)
            pe.wait_ge(copied, (GROUPS - 1) * 4)
            for h in range(2):
                last = nc.tensor.matmul(bank[0][:, 0, :], cg[:, 0, h, :], pg[:, 0, h, :],
                                        start=(h == 0), stop=(h == 1))
            last.then_inc(summed, 1)

        @block.scalar
        def _(act):
            def copy_out(g, b):
                act.wait_ge(summed, g + 1)
                if isinstance(g, int):
                    wait(act, stored[b % 2], 32 * (g // 2))
                else:
                    act.wait_ge(stored[b % 2], g * 16 - 16 * (b % 2))
                for j in range(4):
                    nc.scalar.copy(stage[:, b % 2, 2 * j:2 * j + 2, :],
                                   bank[(b % 2) * 4 + j][:, :, :]).then_inc(copied, 1)
                act.wait_ge(copied, g * 4 + 4)
                for c in range(2):
                    act.dma_start(spec[:, bass.ds(g * GM + c * NLAT, GM), :],
                                  stage[c * NB:(c + 1) * NB, b % 2]).then_inc(stored[b % 2], 16)

            for b in range(RING1):
                copy_out(b, b)
            with nc.scalar.Fori(RING1, GROUPS - RING1 + 1, RING1) as g0:
                for b in range(RING1):
                    copy_out(g0 + b, b)
            act.wait_ge(summed, GROUPS + 1)
            act.wait_ge(stored[0], 32 * (GROUPS // 2))
            nc.scalar.copy(stage[:, 0, 0, :], bank[0][:, 0, :]).then_inc(copied, 1)
            act.wait_ge(copied, GROUPS * 4 + 1)
            act.dma_start(spec[:, NLAT, :], stage[0:NB, 0, 0, :]).then_inc(stored[0], 16)
            act.wait_ge(stored[0], 32 * (GROUPS // 2) + 16)
            act.wait_ge(stored[1], 32 * (GROUPS // 2))

        @block.gpsimd
        def _(pool):
            pool.wait_ge(rec_filled, 2)
            view = recs.rearrange("(p q r) w -> p q r w", p=P, r=32)
            for q in range(4):
                pool.dma_start(view[:, q], rec0[:, :, :]).then_inc(rec_stored, 16)
            pool.wait_ge(rec_stored, 64)


def stage2_blocks(nc, ctx0, K_in, temp_in, bias_in, dft_in, band_in, weight16_in, row_in, tri_in, ident_in,
                  spec, recs, out, count_i):
    with ExitStack() as ctx:
        def sb(name, shape, dt=F32):
            return ctx.enter_context(nc.sbuf_tensor(name, shape, dt))

        def sem(name):
            return ctx.enter_context(nc.semaphore(name))

        dft = sb("dft", [P, 4, HALF])
        Kf = sb("Kf", [P, CH, NLON])
        Khi = sb("Khi", [P, CH, NLON], F32R)
        Klo = sb("Klo", [P, CH, NLON], F32R)
        band = sb("band", [P, TILES, NLAT])
        w16 = sb("w16", [P, 64])
        tri = sb("tri", [P, P])
        ones = sb("ones", [P, P])
        ident = sb("ident", [P, P])
        temp = sb("temp", [P, 1])
        bias = sb("bias", [P, 1])
        mhalf = sb("mhalf", [P, TILES])
        xt = sb("xt", [P, 4, 4, NLAT])
        od = sb("od", [P, TILES, HALF])
        h = sb("h", [P, 4, TILES, NLON])
        xn = sb("xn", [P, 2, TILES, NLON])
        xnhi = sb("xnhi", [P, 4, TILES, NLON], F32R)
        xnlo = sb("xnlo", [P, 4, TILES, NLON], F32R)
        xThi = sb("xThi", [P, 2, CH, NLAT], F32R)
        xTlo = sb("xTlo", [P, 2, CH, NLAT], F32R)
        keyhi = sb("keyhi", [P, CH, NLAT], F32R)
        keylo = sb("keylo", [P, CH, NLAT], F32R)
        th = sb("th", [P, TILES, NLAT])
        lg = sb("lg", [P, TILES, NLAT])
        pr = sb("pr", [P, TILES, NLAT])
        pThi = sb("pThi", [P, TILES, NLAT], F32R)
        pTlo = sb("pTlo", [P, TILES, NLAT], F32R)
        h2 = sb("h2", [P, 2, TILES, NLON])
        o = sb("o", [P, 2, TILES, NLON])
        x2 = sb("x2", [P, 2, TILES, P])
        wb = sb("wb", [P, TILES, 64])
        v4 = sb("v4", [P, 2, TILES * 4])
        rec = sb("rec", [P, 4, TILES, ROW])
        bn1 = sb("bn1", [P, TILES, 6])
        bn2 = sb("bn2", [P, TILES, 6])
        mv1 = sb("mv1", [P, 4, TILES, 2])
        mv2 = sb("mv2", [P, 2, TILES, 2])
        ve = sb("ve", [P, 2, TILES])
        rstd1 = sb("rstd1", [P, 4, TILES])
        rstd2 = sb("rstd2", [P, 2, TILES])
        sc2 = sb("sc2", [P, 2, TILES])
        sh2 = sb("sh2", [P, 2, TILES])
        mx = sb("mx", [P, TILES])
        nmx = sb("nmx", [P, TILES])
        ssum = sb("ssum", [P, 2, TILES])
        rsum = sb("rsum", [P, TILES])
        above = sb("above", [P, TILES, 2])
        mask3 = sb("mask3", [P, 2, 3])
        acc3 = sb("acc3", [P, 2, 3])
        pos = sb("pos", [P, 2, 3])
        nom = sb("nom", [P, TILES])
        fidx = sb("fidx", [P, TILES])
        idx = sb("idx", [P, 4, TILES], U32)
        rows = sb("rows", [P, TILES])

        ps_dft = [ctx.enter_context(nc.psum_tensor(f"ps_dft{i}", [P, NLON], F32)) for i in range(2)]
        ps_kx = [ctx.enter_context(nc.psum_tensor(f"ps_kx{i}", [P, NLON], F32)) for i in range(2)]
        ps_av = [ctx.enter_context(nc.psum_tensor(f"ps_av{i}", [P, NLON], F32)) for i in range(2)]
        ps_l = ctx.enter_context(nc.psum_tensor("ps_l", [P, TILES, NLAT], F32))
        ps_pT = ctx.enter_context(nc.psum_tensor("ps_pT", [P, TILES, NLAT], F32))

        const_loaded = sem("const_loaded")
        k_hi = sem("k_hi")
        k_lo = sem("k_lo")
        consts_set = sem("consts_set")
        x_loaded = [sem(f"x_loaded{i}") for i in range(4)]
        out_stored = [sem(f"out_stored{i}") for i in range(2)]
        pe_dft = sem("pe_dft")
        pe_xT = sem("pe_xT")
        pe_key = sem("pe_key")
        pe_logit = sem("pe_logit")
        pe_pT = sem("pe_pT")
        pe_av = sem("pe_av")
        pe_rank = sem("pe_rank")
        act_od = sem("act_od")
        act_xnhi = sem("act_xnhi")
        act_xThi = sem("act_xThi")
        act_keyhi = sem("act_keyhi")
        act_tanh = sem("act_tanh")
        act_exp = sem("act_exp")
        act_pThi = sem("act_pThi")
        act_out = sem("act_out")
        act_pos = sem("act_pos")
        dve_h = sem("dve_h")
        dve_bn1 = sem("dve_bn1")
        dve_mv1 = sem("dve_mv1")
        dve_xn = sem("dve_xn")
        dve_xnlo = sem("dve_xnlo")
        dve_xTlo = sem("dve_xTlo")
        dve_keylo = sem("dve_keylo")
        dve_max = sem("dve_max")
        dve_pTlo = sem("dve_pTlo")
        dve_rsum = sem("dve_rsum")
        dve_h2 = sem("dve_h2")
        dve_bn2 = sem("dve_bn2")
        dve_mv2 = sem("dve_mv2")
        dve_x2 = sem("dve_x2")
        dve_wb = sem("dve_wb")
        dve_v4 = sem("dve_v4")
        pool_l = sem("pool_l")
        pool_nmx = sem("pool_nmx")
        pool_ve = sem("pool_ve")
        pool_rstd1 = sem("pool_rstd1")
        pool_rstd2 = sem("pool_rstd2")
        pool_sc2 = sem("pool_sc2")
        pool_above = sem("pool_above")
        pool_mask = sem("pool_mask")
        pool_idx = sem("pool_idx")
        pool_rec = sem("pool_rec")
        rec_sent = [sem(f"rec_sent{i}") for i in range(4)]
        cnt_stored = sem("cnt_stored")

        block = ctx.enter_context(nc.Block())

        CONSTS = 11

        FIRST, LAST = -2, NB + 2
        LOOP = (7, NB - 5)

        def settled(eng):
            eng.nop(nofuse=True)

        def slots(eng, slot):
            for i in range(FIRST, LOOP[0]):
                slot(i, i % 4, lambda n: 0 <= n < NB)
            with eng.Fori(LOOP[0], LOOP[1] - 3, 4) as i0:
                for u in range(4):
                    slot(i0 + u, (LOOP[0] + u) % 4, lambda n: True)
            for i in range(LOOP[1], LAST + 1):
                slot(i, i % 4, lambda n: 0 <= n < NB)

        @block.sync
        def _(sp):
            for dst, src in ((dft[:, :, :], dft_in), (Kf[:, :, :], K_in), (band[:, :, :], band_in),
                             (w16[:, :], weight16_in), (tri[:, :], tri_in), (ident[:, :], ident_in),
                             (temp[:, :], temp_in.to_broadcast([P, 1])), (bias[:, :], bias_in.to_broadcast([P, 1])),
                             (rows[:, :], row_in)):
                sp.dma_start(dst, src).then_inc(const_loaded, 16)

            def load(n, k):
                sp.dma_start(xt[:, k].rearrange("p (h q) w -> p h (q w)", h=2),
                             spec[n].rearrange("(h p q) w -> p h (q w)", h=2, q=2)).then_inc(x_loaded[k], 16)

            for n in range(4):
                load(n, n)

            def slot(i, k, has):
                if has(i + 6):
                    sp.wait_ge(pe_dft, (i + 2) * 2 + 2)
                    load(i + 6, (k + 2) % 4)
                if has(i - 2):
                    sp.wait_ge(act_out, (i - 2) * 2 + 2)
                    sp.dma_start(out[i - 2].rearrange("(t p) w -> p t w", p=P),
                                 o[:, k % 2]).then_inc(out_stored[k % 2], 16)

            for i in range(FIRST, LOOP[0]):
                slot(i, i % 4, lambda n: 0 <= n < NB)
            with nc.sync.Fori(LOOP[0], LOOP[1] - 7, 4) as i0:
                for u in range(4):
                    slot(i0 + u, (LOOP[0] + u) % 4, lambda n: True)
            for i in range(LOOP[1] - 4, LAST + 1):
                slot(i, i % 4, lambda n: 0 <= n < NB)
            sp.wait_ge(out_stored[0], 16 * NB // 2)
            sp.wait_ge(out_stored[1], 16 * NB // 2)

        @block.tensor
        def _(pe):
            def product3(out_ap, pairs):
                n = len(pairs)
                for j, (whi, wlo, mhi, mlo) in enumerate(pairs):
                    nc.tensor.matmul(out_ap, whi, mhi, start=(j == 0), stop=False)
                    nc.tensor.matmul(out_ap, whi, mlo, start=False, stop=False)
                    last = nc.tensor.matmul(out_ap, wlo, mhi, start=False, stop=(j == n - 1))
                return last

            def keys(i, k):
                pe.wait_ge(dve_xTlo, i * 2 + 2)
                pe.wait_ge(act_xThi, i * 2 + 2)
                for b in range(2):
                    for e in (2 * b, 2 * b + 1):
                        last = product3(ps_kx[b][:, (e % 2) * NLAT:(e % 2 + 1) * NLAT],
                                        [(Khi[:, d, e * P:(e + 1) * P], Klo[:, d, e * P:(e + 1) * P],
                                          xThi[:, k % 2, d, :], xTlo[:, k % 2, d, :]) for d in range(CH)])
                    last.then_inc(pe_key, 1)

            def probs_T(n):
                pe.wait_ge(act_exp, n * 2 + 2)
                wait(pe, dve_pTlo, n)
                for t in range(TILES):
                    for s in range(TILES):
                        last = nc.tensor.transpose(ps_pT[:, s, t * P:(t + 1) * P],
                                                   pr[:, t, s * P:(s + 1) * P], ident[:, :])
                last.then_inc(pe_pT, 1)

            def inverse_dft(n, k):
                pe.wait_ge(x_loaded[k], n * 4 + (16 - 4 * k))
                for t in range(TILES):
                    wait(pe, dve_h, (n - 1) * 4 + 2 * t + 2)
                    for q in range(2):
                        for c in range(2):
                            last = nc.tensor.matmul(ps_dft[t][:, q * HALF:(q + 1) * HALF],
                                                    xt[:, k, c * 2 + q, t * P:(t + 1) * P],
                                                    dft[:, c * 2 + q, :], start=(c == 0), stop=(c == 1))
                    last.then_inc(pe_dft, 1)

            def attend(n, k):
                pe.wait_ge(act_pThi, n + 1)
                pe.wait_ge(dve_pTlo, n + 1)
                pe.wait_ge(act_xnhi, n + 1)
                pe.wait_ge(dve_xnlo, n + 1)
                for t in range(TILES):
                    wait(pe, dve_h2, (n - 1) * 2 + t + 1)
                    product3(ps_av[t][:, :],
                             [(pThi[:, s, t * P:(t + 1) * P], pTlo[:, s, t * P:(t + 1) * P],
                               xnhi[:, k, s, :], xnlo[:, k, s, :]) for s in range(TILES)]).then_inc(pe_av, 1)

            def rank(n, k):
                pe.wait_ge(pool_mask, n * 4 + 4)
                pe.wait_ge(act_tanh, n + 2 if not isinstance(n, int) else min(n + 2, NB))
                nc.tensor.matmul(ps_l[:, 0, 0:3], tri[:, :], mask3[:, k % 2, :], start=True, stop=False)
                nc.tensor.matmul(ps_l[:, 0, 0:3], ones[:, :], acc3[:, k % 2, :],
                                 start=False, stop=True).then_inc(pe_rank, 1)

            def x_T(n, k):
                pe.wait_ge(dve_xn, n * 2 + 2)
                wait(pe, dve_keylo, n * 2)
                wait(pe, act_keyhi, n * 2)
                for t in range(TILES):
                    for d in range(CH):
                        last = nc.tensor.transpose(ps_kx[t][:, d * P:(d + 1) * P],
                                                   xn[:, k % 2, t, d * P:(d + 1) * P], ident[:, :])
                    last.then_inc(pe_xT, 1)

            def logits(i, k):
                pe.wait_ge(dve_keylo, i * 2 + 2)
                pe.wait_ge(act_keyhi, i * 2 + 2)
                wait(pe, act_tanh, i)
                wait(pe, act_pos, i - 1)
                for t in range(TILES):
                    last = product3(ps_l[:, t, :],
                                    [(keyhi[:, e, t * P:(t + 1) * P], keylo[:, e, t * P:(t + 1) * P],
                                      xThi[:, k % 2, e, :], xTlo[:, k % 2, e, :]) for e in range(CH)])
                last.then_inc(pe_logit, 1)

            def slot(i, k, has):
                if has(i):
                    keys(i, k)
                if has(i - 1):
                    probs_T(i - 1)
                if has(i + 2):
                    inverse_dft(i + 2, (k + 2) % 4)
                if has(i - 1):
                    attend(i - 1, (k + 3) % 4)
                if has(i - 2):
                    rank(i - 2, (k + 2) % 4)
                if has(i + 1):
                    x_T(i + 1, (k + 1) % 4)
                if has(i):
                    logits(i, k)

            pe.wait_ge(const_loaded, 16 * 9)
            pe.wait_ge(k_hi, 1)
            pe.wait_ge(k_lo, 1)
            pe.wait_ge(consts_set, 4)
            slots(nc.tensor, slot)

        @block.scalar
        def _(act):
            def slot(i, k, has):
                if has(i - 1):
                    act.wait_ge(pe_logit, i)
                    wait(act, pool_l, i - 1)
                    nc.scalar.activation(th[:, :, :], ps_l[:, :, :], ACT.Tanh,
                                         bias=bias[:, 0:1]).then_inc(act_tanh, 1)
                    act.wait_ge(pool_nmx, i)
                    wait(act, pe_pT, i - 1)
                    wait(act, dve_rsum, i - 3)
                    for t in range(TILES):
                        nc.scalar.activation(pr[:, t, :], lg[:, t, :], ACT.Exp, bias=nmx[:, t:t + 1],
                                             accum_out=ssum[:, (k + 1) % 2, t:t + 1]).then_inc(act_exp, 1)
                if has(i):
                    for b in range(2):
                        act.wait_ge(pe_key, i * 2 + b + 1)
                        wait(act, pe_logit, i)
                        nc.scalar.copy(keyhi[:, 2 * b:2 * b + 2, :].rearrange("p e w -> p (e w)"),
                                       ps_kx[b][:, :]).then_inc(act_keyhi, 1)
                if has(i - 1):
                    act.wait_ge(pe_pT, i)
                    wait(act, pe_av, (i - 1) * 2)
                    nc.scalar.copy(pThi[:, :, :], ps_pT[:, :, :]).then_inc(act_pThi, 1)
                if has(i + 1):
                    n = i + 1
                    act.wait_ge(dve_xn, n * 2 + 2)
                    wait(act, pe_av, (n - 3) * 2)
                    nc.scalar.copy(xnhi[:, (k + 1) % 4], xn[:, (k + 1) % 2]).then_inc(act_xnhi, 1)
                if has(i - 2):
                    n = i - 2
                    act.wait_ge(pool_sc2, n * 3 + 3)
                    act.wait_ge(dve_h2, n * 2 + 2)
                    wait(act, pool_rec, (n - 1) * 4)
                    if isinstance(n, int):
                        wait(act, out_stored[k % 2], 16 * (n // 2))
                    else:
                        act.wait_ge(out_stored[k % 2], n * 8 - 8 * (k % 2))
                    for t in range(TILES):
                        nc.scalar.activation(o[:, k % 2, t], h2[:, k % 2, t], ACT.Identity,
                                             bias=sh2[:, k % 2, t:t + 1],
                                             scale=sc2[:, k % 2, t:t + 1]).then_inc(act_out, 1)
                if has(i + 2):
                    n = i + 2
                    for t in range(TILES):
                        act.wait_ge(pe_dft, n * 2 + t + 1)
                        wait(act, dve_h, (n - 1) * 4 + 2 * t + 2)
                        nc.scalar.copy(od[:, t, :], ps_dft[t][:, HALF:NLON]).then_inc(act_od, 1)
                if has(i - 2):
                    n = i - 2
                    act.wait_ge(pe_rank, n + 1)
                    wait(act, pool_idx, (n - 1) * 3)
                    nc.scalar.copy(pos[:, k % 2, :], ps_l[:, 0, 0:3]).then_inc(act_pos, 1)
                if has(i + 1):
                    n = i + 1
                    for t in range(TILES):
                        act.wait_ge(pe_xT, n * 2 + t + 1)
                        wait(act, pe_logit, n - 1)
                        nc.scalar.copy(xThi[:, (k + 1) % 2, :, t * P:(t + 1) * P],
                                       ps_kx[t][:, :].rearrange("p (d w) -> p d w", d=CH)).then_inc(act_xThi, 1)

            act.wait_ge(const_loaded, 16 * 9)
            nc.scalar.copy(Khi[:, :, :], Kf[:, :, :]).then_inc(k_hi, 1)
            slots(nc.scalar, slot)

        @block.vector
        def _(dve):
            def slot(i, k, has):
                if has(i - 1):
                    dve.wait_ge(pool_l, i)
                    wait(dve, pool_nmx, i - 1)
                    for t in range(TILES):
                        nc.vector.tensor_scalar(lg[:, t, :], lg[:, t, :], temp[:, 0:1], None, ALU.mult,
                                                ALU.max, accum_out=mx[:, t:t + 1]).then_inc(dve_max, 1)
                if has(i - 2):
                    n, r4, r2 = i - 2, (k + 2) % 4, k % 2
                    dve.wait_ge(act_exp, n * 2 + 2)
                    nc.vector.reciprocal(rsum[:, :], ssum[:, r2, :]).then_inc(dve_rsum, 1)
                    dve.wait_ge(dve_rsum, n + 1)
                    wait(dve, act_out, (n - 1) * 2)
                    for t in range(TILES):
                        dve.wait_ge(pe_av, n * 2 + t + 1)
                        nc.vector.scalar_tensor_tensor(out=h2[:, r2, t], in0=ps_av[t][:, :],
                                                       scalar=rsum[:, t:t + 1], in1=h[:, r4, t],
                                                       op0=ALU.mult, op1=ALU.add).then_inc(dve_h2, 1)
                    for t in range(TILES):
                        dve.wait_ge(dve_h2, n * 2 + t + 1)
                        wait(dve, dve_mv2, (n - 1) * 2 + t + 1)
                        nc.vector.bn_stats(bn2[:, t, :], h2[:, r2, t]).then_inc(dve_bn2, 1)
                    wait(dve, pool_sc2, (n - 1) * 3)
                    for t in range(TILES):
                        dve.wait_ge(dve_bn2, n * 2 + t + 1)
                        settled(dve)
                        nc.vector.bn_aggr(mv2[:, r2, t, :], bn2[:, t, :]).then_inc(dve_mv2, 1)
                if has(i + 1):
                    n, r4, r2 = i + 1, (k + 1) % 4, (k + 1) % 2
                    dve.wait_ge(pool_rstd1, n + 1)
                    wait(dve, pe_xT, (n - 1) * 2)
                    wait(dve, act_xnhi, n - 1)
                    wait(dve, dve_xnlo, n - 1)
                    for t in range(TILES):
                        nc.vector.tensor_scalar(xn[:, r2, t], h[:, r4, t], mv1[:, r4, t, 0:1],
                                                rstd1[:, r4, t:t + 1], ALU.subtract,
                                                ALU.mult).then_inc(dve_xn, 1)
                if has(i):
                    wait(dve, pe_logit, i)
                    for b in range(2):
                        dve.wait_ge(act_keyhi, i * 2 + b + 1)
                        nc.vector.tensor_tensor(
                            keylo[:, 2 * b:2 * b + 2, :].rearrange("p e w -> p (e w)"), ps_kx[b][:, :],
                            keyhi[:, 2 * b:2 * b + 2, :].bitcast(F32).rearrange("p e w -> p (e w)"),
                            ALU.subtract).then_inc(dve_keylo, 1)
                if has(i - 1):
                    dve.wait_ge(act_pThi, i)
                    wait(dve, pe_av, (i - 1) * 2)
                    nc.vector.tensor_tensor(pTlo[:, :, :], ps_pT[:, :, :], pThi[:, :, :].bitcast(F32),
                                            ALU.subtract).then_inc(dve_pTlo, 1)
                if has(i - 2):
                    n, r2 = i - 2, k % 2
                    dve.wait_ge(pool_rstd2, n + 1)
                    wait(dve, pool_rec, (n - 1) * 4)
                    wait(dve, pool_above, n - 1)
                    for t in range(TILES):
                        nc.vector.tensor_scalar(x2[:, r2, t, :], h2[:, r2, t, 0:P], mv2[:, r2, t, 0:1],
                                                rstd2[:, r2, t:t + 1], ALU.subtract,
                                                ALU.mult).then_inc(dve_x2, 1)
                    dve.wait_ge(dve_x2, n * 2 + 2)
                    wait(dve, dve_v4, n)
                    for t in range(TILES):
                        last = nc.vector.scalar_tensor_tensor(out=wb[:, t, :], in0=x2[:, r2, t, 64:128], scalar=0.5,
                                                              in1=w16[:, :], op0=ALU.is_gt, op1=ALU.mult)
                    last.then_inc(dve_wb, 1)
                    dve.wait_ge(dve_wb, n + 1)
                    nc.vector.tensor_reduce(v4[:, r2, :], wb[:, :, :].rearrange("p t (g w) -> p (t g) w", w=16),
                                            AX_X, ALU.max).then_inc(dve_v4, 1)
                if has(i + 2):
                    n, r4 = i + 2, (k + 2) % 4
                    for t in range(TILES):
                        dve.wait_ge(act_od, n * 2 + t + 1)
                        for s, op in ((0, ALU.add), (1, ALU.subtract)):
                            nc.vector.tensor_tensor(h[:, r4, t, s * HALF:(s + 1) * HALF], ps_dft[t][:, 0:HALF],
                                                    od[:, t, :], op).then_inc(dve_h, 1)
                    for t in range(TILES):
                        dve.wait_ge(dve_h, n * 4 + 2 * t + 2)
                        wait(dve, dve_mv1, (n - 1) * 2 + t + 1)
                        nc.vector.bn_stats(bn1[:, t, :], h[:, r4, t]).then_inc(dve_bn1, 1)
                    wait(dve, pool_rstd1, n - 3)
                    for t in range(TILES):
                        dve.wait_ge(dve_bn1, n * 2 + t + 1)
                        settled(dve)
                        nc.vector.bn_aggr(mv1[:, r4, t, :], bn1[:, t, :]).then_inc(dve_mv1, 1)
                if has(i + 1):
                    n, r4, r2 = i + 1, (k + 1) % 4, (k + 1) % 2
                    dve.wait_ge(act_xnhi, n + 1)
                    wait(dve, pe_av, (n - 3) * 2)
                    nc.vector.tensor_tensor(xnlo[:, r4], xn[:, r2], xnhi[:, r4].bitcast(F32),
                                            ALU.subtract).then_inc(dve_xnlo, 1)
                    wait(dve, pe_logit, n - 1)
                    for t in range(TILES):
                        dve.wait_ge(act_xThi, n * 2 + t + 1)
                        nc.vector.tensor_tensor(xTlo[:, r2, :, t * P:(t + 1) * P],
                                                ps_kx[t][:, :].rearrange("p (d w) -> p d w", d=CH),
                                                xThi[:, r2, :, t * P:(t + 1) * P].bitcast(F32),
                                                ALU.subtract).then_inc(dve_xTlo, 1)

            nc.vector.memset(ones[:, :], 1.0).then_inc(consts_set, 1)
            nc.vector.memset(mhalf[:, :], -0.5).then_inc(consts_set, 1)
            nc.vector.memset(mask3[:, :, :], 0.0).then_inc(consts_set, 1)
            nc.vector.memset(acc3[:, :, :], 0.0).then_inc(consts_set, 1)
            nc.vector.memset(rec[:, :, :, :], 0.0).then_inc(consts_set, 1)
            dve.wait_ge(const_loaded, 16 * 9)
            dve.wait_ge(k_hi, 1)
            nc.vector.tensor_tensor(Klo[:, :, :], Kf[:, :, :], Khi[:, :, :].bitcast(F32),
                                    ALU.subtract).then_inc(k_lo, 1)
            slots(nc.vector, slot)

        @block.gpsimd
        def _(pool):
            def slot(i, k, has):
                if has(i - 1):
                    pool.wait_ge(act_tanh, i)
                    wait(pool, act_exp, (i - 1) * 2)
                    nc.gpsimd.tensor_tensor(lg[:, :, :], th[:, :, :], band[:, :, :], ALU.add).then_inc(pool_l, 1)
                    pool.wait_ge(dve_max, i * 2)
                    settled(pool)
                    nc.gpsimd.tensor_scalar(nmx[:, :], mx[:, :], -1.0, None, ALU.mult).then_inc(pool_nmx, 1)
                if has(i - 2):
                    n, r2 = i - 2, k % 2
                    pool.wait_ge(dve_mv2, n * 2 + 2)
                    settled(pool)
                    nc.gpsimd.tensor_scalar(ve[:, 1, :], mv2[:, r2, :, 1], EPS, None, ALU.add).then_inc(pool_ve, 1)
                    pool.wait_ge(pool_ve, n + 1 + (min(n + 4, NB) if isinstance(n, int) else n + 4))
                    nc.gpsimd.tensor_tensor(rstd2[:, r2, :], ve[:, 1, :], mhalf[:, :], ALU.pow).then_inc(pool_rstd2, 1)
                    pool.wait_ge(pool_rstd2, n + 1)
                    wait(pool, act_out, (n - 1) * 2)
                    settled(pool)
                    nc.gpsimd.tensor_scalar(sc2[:, r2, :], rstd2[:, r2, :], 1.0, None, ALU.add).then_inc(pool_sc2, 1)
                    for t in range(TILES):
                        nc.gpsimd.tensor_scalar(sh2[:, r2, t:t + 1], mv2[:, r2, t, 0:1], rstd2[:, r2, t:t + 1], -1.0,
                                                ALU.mult, ALU.mult).then_inc(pool_sc2, 1)
                if has(i - 3):
                    n, r4, r2 = i - 3, (k + 1) % 4, (k + 1) % 2
                    if isinstance(n, int):
                        wait(pool, rec_sent[r4], 32 * (n // 4))
                    else:
                        pool.wait_ge(rec_sent[r4], n * 8 - 8 * r4)
                    pool.wait_ge(dve_v4, n + 1)
                    pool.wait_ge(act_pos, n + 1)
                    settled(pool)
                    nc.gpsimd.tensor_scalar(nom[:, :], mask3[:, r2, 0:2], -FAR, FAR, ALU.mult,
                                            ALU.add).then_inc(pool_idx, 1)
                    pool.wait_ge(pool_idx, n * 3 + 1)
                    nc.gpsimd.tensor_tensor(fidx[:, :], pos[:, r2, 0:2], nom[:, :], ALU.add).then_inc(pool_idx, 1)
                    pool.wait_ge(pool_idx, n * 3 + 2)
                    settled(pool)
                    nc.gpsimd.tensor_copy(idx[:, r4, :], fidx[:, :]).then_inc(pool_idx, 1)
                    nc.gpsimd.tensor_copy(rec[:, r4, :, 0], rows[:, :]).then_inc(pool_rec, 1)
                    nc.gpsimd.tensor_copy(rec[:, r4, :, 1:5],
                                          v4[:, r2, :].rearrange("p (t g) -> p t g", t=TILES)).then_inc(pool_rec, 1)
                    nc.gpsimd.tensor_copy(rec[:, r4, :, 5], x2[:, r2, :, 29]).then_inc(pool_rec, 1)
                    pool.wait_ge(act_out, n * 2 + 2)
                    settled(pool)
                    nc.gpsimd.tensor_copy(rec[:, r4, :, 8:ROW],
                                          o[:, r2, :, OUT_LO:OUT_LO + OUT_W]).then_inc(pool_rec, 1)
                    pool.wait_ge(pool_rec, n * 4 + 4)
                    pool.wait_ge(pool_idx, n * 3 + 3)
                    settled(pool)
                    nc.gpsimd.tensor_scalar(rows[:, :], rows[:, :], float(NLAT * 16), None, ALU.add)
                    for t in range(TILES):
                        nc.gpsimd.indirect_dma_start(
                            out=recs[:, :], out_offset=bass.IndirectOffsetOnAxis(ap=idx[:, r4, t:t + 1], axis=0),
                            in_=rec[:, r4, t, :], in_offset=None, bounds_check=NB * NLAT - 1,
                            oob_is_err=False).then_inc(rec_sent[r4], 16)
                if has(i - 2):
                    n, r2 = i - 2, k % 2
                    pool.wait_ge(dve_x2, n * 2 + 2)
                    settled(pool)
                    nc.gpsimd.tensor_scalar(above[:, :, :], x2[:, r2, :, 0:2], 0.5, None, ALU.is_ge).then_inc(pool_above, 1)
                    pool.wait_ge(pool_above, n + 1)
                    nc.gpsimd.tensor_tensor(mask3[:, r2, 0:2], above[:, :, 0], above[:, :, 1], ALU.mult).then_inc(pool_mask, 1)
                    nc.gpsimd.tensor_copy(acc3[:, r2, 0:1], acc3[:, 1 - r2, 2:3]).then_inc(pool_mask, 1)
                    pool.wait_ge(pool_mask, n * 4 + 2)
                    nc.gpsimd.tensor_tensor(acc3[:, r2, 1:2], acc3[:, r2, 0:1], mask3[:, r2, 0:1],
                                            ALU.add).then_inc(pool_mask, 1)
                    pool.wait_ge(pool_mask, n * 4 + 3)
                    nc.gpsimd.tensor_tensor(acc3[:, r2, 2:3], acc3[:, r2, 1:2], mask3[:, r2, 1:2],
                                            ALU.add).then_inc(pool_mask, 1)
                    if not isinstance(n, int) or n + 1 < NB:
                        pool.wait_ge(pool_mask, n * 4 + 4)
                if has(i + 2):
                    n, r4 = i + 2, (k + 2) % 4
                    pool.wait_ge(dve_mv1, n * 2 + 2)
                    settled(pool)
                    nc.gpsimd.tensor_scalar(ve[:, 0, :], mv1[:, r4, :, 1], EPS, None, ALU.add).then_inc(pool_ve, 1)
                    pool.wait_ge(pool_ve, (max(n - 3, 0) if isinstance(n, int) else n - 3) + n + 1)
                    wait(pool, dve_xn, (n - 3) * 2)
                    nc.gpsimd.tensor_tensor(rstd1[:, r4, :], ve[:, 0, :], mhalf[:, :], ALU.pow).then_inc(pool_rstd1, 1)

            pool.wait_ge(const_loaded, 16 * 9)
            pool.wait_ge(consts_set, 5)
            slots(nc.gpsimd, slot)
            for r in range(4):
                pool.wait_ge(rec_sent[r], 32 * (NB // 4))
            nc.gpsimd.tensor_copy(count_i[:, :], pos[:, (NB - 1) % 2, 2:3])


def stage3_ffn(nc, W1_in, Wm_in, W7_in, bias_in, sel_in, iota_in, ident_in, recs, out, count_i):
    with ExitStack() as ctx:
        def sb(name, shape, dt=F32):
            return ctx.enter_context(nc.sbuf_tensor(name, shape, dt))

        def sem(name):
            return ctx.enter_context(nc.semaphore(name))

        W1f = sb("W1f", [64, 6, P])
        W1h = sb("W1h", [64, 6, P], F32R)
        W1l = sb("W1l", [64, 6, P])
        W1 = sb("W1", [64, 6, P], F32R)
        Wf = sb("Wf", [P, MID, WCOLS])
        Whi = sb("Whi", [P, MID, WCOLS], F32R)
        Wlo = sb("Wlo", [P, MID, WCOLS], F32R)
        W7 = sb("W7", [P, 5])
        fb = sb("fb", [P, 13])
        sel = sb("sel", [64, 2])
        iota = sb("iota", [P, 16])
        ident = sb("ident3", [P, P])
        rt = sb("rt", [P, 1, TJ, ROW])
        n16 = sb("n16", [P, TJ, 4])
        oph = sb("oph", [P, TJ], F32R)
        feat = sb("feat", [P, TJ, 64])
        xin = sb("xin", [64, TJ * P], F32R)
        act_f = sb("act_f", [P, 2, 5, 512])
        act_hi = sb("act_hi", [P, 2, 5, 512], F32R)
        act_lo = sb("act_lo", [P, 2, 5, 512], F32R)
        res = sb("res", [P, 4, 2 * TJ])
        hot = sb("hot", [P, 2 * TJ, 16])
        oc = sb("oc", [P, TJ, OUT_W])
        dest = sb("dest", [P, TJ], U32)

        ps_main = [ctx.enter_context(nc.psum_tensor(f"ps_main{i}", [P, 512], F32)) for i in range(5)]
        ps_x = [ctx.enter_context(nc.psum_tensor(f"ps_x{i}", [P, 512], F32)) for i in range(2)]
        ps_y = ctx.enter_context(nc.psum_tensor("ps_y", [P, 2 * TJ], F32))

        w_loaded = sem("w_loaded")
        w_hi = sem("w_hi")
        w_lo = sem("w_lo")
        w1_lo = sem("w1_lo")
        feat_zero = sem("feat_zero")
        rec_loaded = sem("rec_loaded")
        rec_used = sem("rec_used")
        oc_free = sem("oc_free")
        feat_part = sem("feat_part")
        feat_made = sem("feat_made")
        feat_T = sem("feat_T")
        xin_made = sem("xin_made")
        pe_layer = sem("pe_layer")
        act_relu = sem("act_relu")
        dve_relu = sem("dve_relu")
        dve_relo = sem("dve_relo")
        pe_y = sem("pe_y")
        dve_res = sem("dve_res")
        dve_hot = sem("dve_hot")
        scattered = sem("scattered")

        block = ctx.enter_context(nc.Block())
        LAYERS = MID + 1
        order = (0, 1, 2, 3, 4)

        def steps(eng, body):
            count = eng.value_load(count_i[0:1, 0:1], min_val=0, max_val=NB * NLAT)
            with eng.Fori(0, NB * NLAT // (TJ * P)) as s:
                with eng.If(count > s * (TJ * P)):
                    body(s)

        @block.sync
        def _(sp):
            for dst, src in ((W1f[:, :, :], W1_in), (Wf[:, :, :], Wm_in), (W7[:, :], W7_in), (fb[:, :], bias_in),
                             (sel[:, :], sel_in), (iota[:, :], iota_in), (ident[:, :], ident_in)):
                sp.dma_start(dst, src).then_inc(w_loaded, 16)

            def body(s):
                sp.wait_ge(rec_used, s + 1)
                sp.dma_start(rt[:, 0], recs[bass.ds(s * (TJ * P), TJ * P), :]
                             .rearrange("(p j) w -> p j w", p=P)).then_inc(rec_loaded, 16)

            steps(nc.sync, body)

        @block.vector
        def _(dve):
            nc.vector.memset(feat[:, :, :], 0.0).then_inc(feat_zero, 1)
            nc.vector.memset(rt[:, 0], 0.0).then_inc(rec_used, 1)
            dve.wait_ge(w_loaded, 16 * 7)
            dve.wait_ge(w_hi, 2)
            nc.vector.tensor_tensor(Wlo[:, :, :], Wf[:, :, :], Whi[:, :, :].bitcast(F32), ALU.subtract).then_inc(w_lo, 1)
            nc.vector.tensor_tensor(W1l[:, :, :], W1f[:, :, :], W1h[:, :, :].bitcast(F32), ALU.subtract).then_inc(w1_lo, 1)
            dve.wait_ge(w1_lo, 1)
            nc.vector.tensor_scalar(W1l[:, :, :], W1l[:, :, :], sel[:, 1:2], None, ALU.mult).then_inc(w1_lo, 1)
            dve.wait_ge(w1_lo, 2)
            nc.vector.scalar_tensor_tensor(
                out=W1[:, :, :].rearrange("p a b -> p (a b)"), in0=W1h[:, :, :].bitcast(F32).rearrange("p a b -> p (a b)"),
                scalar=sel[:, 0:1], in1=W1l[:, :, :].rearrange("p a b -> p (a b)"), op0=ALU.mult, op1=ALU.add).then_inc(w_lo, 1)
            dve.wait_ge(feat_zero, 1)

            def body(s):
                r = rt[:, 0]
                v = r[:, :, 1:5]
                dve.wait_ge(rec_loaded, s * 16 + 16)
                nc.vector.tensor_scalar(n16[:, :, :], v, 0.0, 16.0, ALU.is_gt, ALU.mult).then_inc(feat_part, 1)
                nc.vector.tensor_copy(oph[:, :], r[:, :, 5]).then_inc(feat_part, 1)
                dve.wait_ge(feat_part, s * 2 + 2)
                f4 = feat[:, :, :].rearrange("p j (q w) -> p j q w", q=2)
                for at in (0, 4):
                    nc.vector.tensor_tensor(f4[:, :, :, at:at + 2], n16[:, :, :].rearrange("p j (b q) -> p j q b", q=2),
                                            v.rearrange("p j (b q) -> p j q b", q=2), ALU.subtract).then_inc(feat_made, 1)
                high = oph[:, :].bitcast(F32).unsqueeze(2).to_broadcast([P, TJ, 2])
                for at in (2, 6):
                    nc.vector.tensor_copy(f4[:, :, :, at], high).then_inc(feat_made, 1)
                nc.vector.tensor_tensor(f4[:, :, :, 3], r[:, :, 5].unsqueeze(2).to_broadcast([P, TJ, 2]), high,
                                        ALU.subtract).then_inc(feat_made, 1)
                for L in range(LAYERS):
                    for i, g in enumerate(order):
                        done = s * (5 * LAYERS) + (5 * L + i + 1)
                        dve.wait_ge(pe_layer, done)
                        if L < LAYERS - 1:
                            dve.wait_ge(act_relu, s * (5 * MID) + (5 * L + i + 1))
                        col = (L if g < 4 else 6 + L)
                        nc.vector.tensor_scalar(act_f[:, L % 2, g], ps_main[g][:, :], fb[:, col:col + 1], 0.0,
                                                ALU.add, ALU.max).then_inc(dve_relu, 1)
                        if L < LAYERS - 1:
                            dve.wait_ge(dve_relu, done)
                            nc.vector.tensor_tensor(act_lo[:, L % 2, g], act_f[:, L % 2, g],
                                                    act_hi[:, L % 2, g].bitcast(F32), ALU.subtract).then_inc(dve_relo, 1)
                dve.wait_ge(pe_y, s + 1)
                nc.vector.tensor_scalar(res[:, 0], ps_y[:, :], fb[:, 12:13], -1.0, ALU.add, ALU.max).then_inc(dve_res, 1)
                dve.wait_ge(dve_res, s * 4 + 1)
                nc.vector.tensor_scalar(res[:, 1], res[:, 0], 16.0, MAGIC, ALU.min, ALU.add).then_inc(dve_res, 1)
                dve.wait_ge(dve_res, s * 4 + 2)
                nc.vector.tensor_scalar(res[:, 2], res[:, 1], -MAGIC, 0.0, ALU.add, ALU.max).then_inc(dve_res, 1)
                dve.wait_ge(dve_res, s * 4 + 3)
                nc.vector.tensor_scalar(res[:, 3], res[:, 2], 15.0, None, ALU.min).then_inc(dve_res, 1)
                dve.wait_ge(dve_res, s * 4 + 4)
                nc.vector.tensor_tensor(hot[:, :, :], iota[:, :].unsqueeze(1).to_broadcast([P, 2 * TJ, 16]),
                                        res[:, 3].unsqueeze(2).to_broadcast([P, 2 * TJ, 16]), ALU.is_equal).then_inc(dve_hot, 1)
                dve.wait_ge(dve_hot, s + 1)
                dve.wait_ge(oc_free, s + 1)
                for q in range(2):
                    nc.vector.scalar_tensor_tensor(out=oc[:, :, q * 16:(q + 1) * 16], in0=hot[:, q * TJ:(q + 1) * TJ],
                                                   scalar=2.0, in1=r[:, :, 8 + q * 16:24 + q * 16],
                                                   op0=ALU.mult, op1=ALU.add)
                nc.vector.tensor_copy(dest[:, :], r[:, :, 0]).then_inc(rec_used, 1)

            steps(nc.vector, body)

        @block.scalar
        def _(act):
            act.wait_ge(w_loaded, 16 * 7)
            nc.scalar.copy(Whi[:, :, :], Wf[:, :, :]).then_inc(w_hi, 1)
            nc.scalar.copy(W1h[:, :, :], W1f[:, :, :]).then_inc(w_hi, 1)

            def body(s):
                act.wait_ge(feat_T, s + 1)
                for a in range(2):
                    nc.scalar.copy(xin[:, a * 512:(a + 1) * 512], ps_x[a][0:64, :]).then_inc(xin_made, 1)
                for L in range(LAYERS - 1):
                    for i, g in enumerate(order):
                        act.wait_ge(pe_layer, s * (5 * LAYERS) + (5 * L + i + 1))
                        col = (L if g < 4 else 6 + L)
                        nc.scalar.activation(act_hi[:, L % 2, g], ps_main[g][:, :], ACT.Relu,
                                             bias=fb[:, col:col + 1]).then_inc(act_relu, 1)

            steps(nc.scalar, body)

        @block.tensor
        def _(pe):
            pe.wait_ge(w_loaded, 16 * 7)
            pe.wait_ge(w_lo, 2)

            def body(s):
                pe.wait_ge(feat_made, s * 5 + 5)
                pe.nop(nofuse=True)
                for j in range(TJ):
                    last = nc.tensor.transpose(ps_x[j // 4][0:64, (j % 4) * P:(j % 4 + 1) * P], feat[:, j, :], ident[:, :])
                last.then_inc(feat_T, 1)
                pe.wait_ge(xin_made, s * 2 + 2)
                for g in range(4):
                    nc.tensor.matmul(ps_main[g][:, :], W1[:, g // 2, :], xin[:, (g % 2) * 512:(g % 2 + 1) * 512],
                                     start=True, stop=True).then_inc(pe_layer, 1)
                for g in range(4):
                    last = nc.tensor.matmul(ps_main[4][:, :], W1[:, 2 + g, :], xin[:, (g % 2) * 512:(g % 2 + 1) * 512],
                                            start=(g == 0), stop=(g == 3))
                last.then_inc(pe_layer, 1)

                for L in range(1, LAYERS):
                    src = (L - 1) % 2

                    def ready(i):
                        pe.wait_ge(dve_relo, s * (5 * MID) + (5 * (L - 1) + i + 1))

                    def product(out_ap, lo, hi, cols, g, start, stop):
                        w = L - 1
                        nc.tensor.matmul(out_ap, Whi[lo:hi, w, cols], act_hi[lo:hi, src, g], start=start, stop=False)
                        nc.tensor.matmul(out_ap, Whi[lo:hi, w, cols], act_lo[lo:hi, src, g], start=False, stop=False)
                        return nc.tensor.matmul(out_ap, Wlo[lo:hi, w, cols], act_hi[lo:hi, src, g], start=False, stop=stop)

                    def main(g):
                        ready(g)
                        product(ps_main[g][:, :], 0, P, slice(0, P), g, True, False)

                    def rest(g):
                        product(ps_main[g][:, :], 32 * g, 32 * g + 32, slice(P, 2 * P), 4, False, True).then_inc(pe_layer, 1)

                    main(0)
                    main(1)
                    main(2)
                    ready(4)
                    rest(0)
                    rest(1)
                    rest(2)
                    main(3)
                    rest(3)
                    for g in range(4):
                        at = 2 * P + 96 - 32 * g
                        product(ps_main[4][:, :], 0, P, slice(at, at + P), g, g == 0, False)
                    product(ps_main[4][:, :], 0, P, slice(2 * P + 224, 3 * P + 224), 4, False, True).then_inc(pe_layer, 1)
                pe.wait_ge(dve_relu, s * (5 * LAYERS) + 5 * LAYERS)
                for q in range(2):
                    for j in range(TJ):
                        g = q * 2 + j // 4
                        c = slice((j % 4) * P, (j % 4 + 1) * P)
                        a = (LAYERS - 1) % 2
                        nc.tensor.matmul(ps_y[:, q * TJ + j:q * TJ + j + 1], act_f[:, a, g, c], W7[:, 0:1],
                                         start=True, stop=False)
                        last = nc.tensor.matmul(ps_y[:, q * TJ + j:q * TJ + j + 1], act_f[:, a, 4, c], W7[:, 1 + g:2 + g],
                                                start=False, stop=True)
                last.then_inc(pe_y, 1)

            steps(nc.tensor, body)

        @block.gpsimd
        def _(pool):
            nc.gpsimd.memset(oc[:, :, :], 0.0).then_inc(oc_free, 1)
            out_rows = out.rearrange("n k (g w) -> (n k g) w", w=OUT_W)

            def body(s):
                pool.wait_ge(rec_used, s + 2)
                pool.nop(nofuse=True)
                for j in range(TJ):
                    nc.gpsimd.indirect_dma_start(
                        out=out_rows, out_offset=bass.IndirectOffsetOnAxis(ap=dest[:, j:j + 1], axis=0),
                        in_=oc[:, j, :], in_offset=None, bounds_check=NB * NLAT * (NLON // OUT_W) - 1,
                        oob_is_err=False).then_inc(scattered, 16)
                pool.wait_ge(scattered, s * (16 * TJ) + 16 * TJ)
                pool.sem_inc(oc_free, 1)

            steps(nc.gpsimd, body)


def build(nc, xs, pct, se, K, temp, bias, W1, Wm, W7, fb, dft, band, w16, row, tri, ident, sel, iota, out):
    ctx = ExitStack()
    with ctx:
        spec = nc.dram_tensor("spec", (NB, 2 * NLAT, NLAT), F32, kind="Internal").ap()
        recs = nc.dram_tensor("recs", (NB * NLAT, ROW), F32, kind="Internal").ap()
        count_i = ctx.enter_context(nc.sbuf_tensor("count_i", [P, 1], U32))
        stage1_spectrum(nc, ctx, xs, pct, se, spec, recs)
        stage2_blocks(nc, ctx, K, temp, bias, dft, band, w16, row, tri, ident, spec, recs, out, count_i)
        stage3_ffn(nc, W1, Wm, W7, fb, sel, iota, ident, recs, out, count_i)


def constants():
    p = np.arange(P)[:, None].astype(np.float64)
    j = np.arange(HALF)[None, :].astype(np.float64)
    dft = np.zeros((P, 4, HALF))
    for q in range(2):
        m = 2 * p + q
        angle = 2 * np.pi * np.mod(m * j, NLON) / NLON
        dft[:, q] = np.where(m == 0, 1.0, 2.0) * np.cos(angle)
        dft[:, 2 + q] = -2.0 * np.sin(angle)
    dft[0, 2] = np.cos(np.pi * j[0])
    q = np.arange(NLAT)[:, None]
    t = np.arange(NLAT)[None, :]
    inside = (q - 6 <= t) & (t < q + 6)
    band = np.where(inside, 0.0, -10000.0).reshape(TILES, P, NLAT).transpose(1, 0, 2)
    w16 = np.tile(16.0 - np.arange(16), 4)[None, :].repeat(P, 0)
    row = (np.arange(TILES)[None, :] * P + np.arange(P)[:, None]) * 16.0 + OUT_LO // OUT_W
    tri = (np.arange(P)[:, None] < np.arange(P)[None, :])
    sel = np.zeros((64, 2))
    for at in (0, 32):
        sel[at:at + 4, 0] = 1.0
        sel[at + 4:at + 7, 1] = 1.0
    iota = np.arange(16)[None, :].repeat(P, 0)
    f = lambda a: np.ascontiguousarray(a, dtype=np.float32)
    return dict(dft=f(dft), band=f(band), w16=f(w16), row=f(row), tri=f(tri), ident=f(np.eye(P)),
                sel=f(sel), iota=f(iota))


def ffn_layout(W, b):
    T = W.transpose(0, 2, 1)
    W1 = np.zeros((64, 6, P), W.dtype)
    for q in range(2):
        for r, d in enumerate((0, 1, 30, 30, 0, 1, 30)):
            W1[32 * q + r, q] = T[0, d, 0:P]
            for g in (2 * q, 2 * q + 1):
                W1[32 * q + r, 2 + g, 32 * g:32 * g + 32] = T[0, d, P:]
    Wm = np.zeros((P, MID, WCOLS), W.dtype)
    for w in range(MID):
        t = T[1 + w]
        Wm[:, w, 0:P] = t[0:P, 0:P]
        for g in range(4):
            Wm[32 * g:32 * g + 32, w, P:2 * P] = t[P:, 0:P]
            Wm[32 * g:32 * g + 32, w, 2 * P + 224 + 32 * g:2 * P + 256 + 32 * g] = t[P:, P:]
        Wm[:, w, 2 * P + 96:2 * P + 128] = t[0:P, P:]
    W7 = np.zeros((P, 5), W.dtype)
    W7[:, 0] = T[6, 0:P, 2]
    fb = np.zeros((P, 13), b.dtype)
    for g in range(4):
        W7[32 * g:32 * g + 32, 1 + g] = T[6, P:, 2]
        fb[32 * g:32 * g + 32, 6:12] = b[0:6, P:].T
    fb[:, 0:6] = b[0:6, 0:P].T
    fb[:, 12] = b[6, 2]
    return dict(W1=W1, Wm=Wm, W7=W7, fb=fb)


def kernel(**inputs):
    import concourse.bacc as _bacc
    from concourse.bass_utils import run_bass_kernel_spmd as _run

    nc = _bacc.Bacc("TRN2", target_bir_lowering=False, num_devices=1)
    x = np.asarray(inputs["x"])
    xs = x.reshape(NB, 2, P, MMAX, 2).transpose(2, 3, 1, 4, 0).reshape(P, MMAX * 2, P)
    pct = np.asarray(inputs["L0_tok_pct"]).reshape(MMAX, 2, P, NLAT).transpose(2, 0, 1, 3).reshape(P, MMAX * 2, NLAT)
    se = np.asarray(inputs["L0_tok_sqrt_eig"])[0].reshape(2, P, MMAX).transpose(1, 2, 0).reshape(P, MMAX * 2)
    K = np.asarray(inputs["L0_attn_K"]).reshape(CH, P, NLON).transpose(1, 0, 2)
    arrays = dict(xs=xs, pct=pct, se=se, K=K,
                  temp=np.asarray(inputs["L0_attn_temperature"]).reshape(1, 1),
                  bias=np.asarray(inputs["L0_attn_bias"]).reshape(1, 1),
                  **ffn_layout(np.asarray(inputs["L0_ffn_W"]), np.asarray(inputs["L0_ffn_b"])), **constants())
    sent, args = {}, []
    for name, a in arrays.items():
        a = np.ascontiguousarray(a)
        sent[f"in_{name}_dram"] = a
        args.append(nc.dram_tensor(f"in_{name}_dram", a.shape, mybir.dt.from_np(a.dtype), kind="ExternalInput").ap())
    args.append(nc.dram_tensor("out_0_dram", (NB, NLAT, NLON), F32, kind="ExternalOutput").ap())
    build(nc, *args)
    r = _run(nc, [sent], core_ids=[0])
    return r.results[0]["out_0_dram"]
```

```python
from contextlib import ExitStack

import numpy as np

import concourse.bass as bass
from concourse import mybir

F32 = mybir.dt.float32
F32R = mybir.dt.float32r
U32 = mybir.dt.uint32
ACT = mybir.ActivationFunctionType
ALU = mybir.AluOpType
AX_X = mybir.AxisListType.X

P = 128
NB, NLAT, MMAX, NLON = 64, 256, 257, 512
TILES = NLAT // P
CH = NLON // P
EPS = 1e-5

GM = 8
GROUPS = (MMAX - 1) // GM
RING1 = 4

ROW = 40
OUT_LO, OUT_W = 128, 32
FAR = 1048576.0
HALF = NLON // 2
Q = NLON // 4
RE_EVEN, IM_EVEN, RE_ODD, IM_ODD, TOP = (0, Q + 1), (Q + 1, 2 * Q), (2 * Q, 3 * Q), (3 * Q, 4 * Q), (4 * Q, 5 * Q + 1)
DFT_COLS = TOP[1]
MID = 5
WCOLS = 3 * P + 224
TJ = 8
MAGIC = 12582912.0


def wait(eng, sem, value):
    if isinstance(value, int) and value <= 0:
        return
    eng.wait_ge(sem, value)


class OnChip:

    def __init__(self, nc, ctx):
        def sb(name, shape, dt=F32):
            return ctx.enter_context(nc.sbuf_tensor(name, shape, dt))

        self.dft = sb("dft", [P, DFT_COLS])
        self.Khi = sb("Khi", [P, CH, NLON], F32R)
        self.Klo = sb("Klo", [P, CH, NLON], F32R)
        self.band = sb("band", [P, TILES, NLAT])
        self.w16 = sb("w16", [P, 64])
        self.tri = sb("tri", [P, P])
        self.ident = sb("ident", [P, P])
        self.temp = sb("temp", [P, 1])
        self.bias = sb("bias", [P, 1])
        self.rows = sb("rows", [P, TILES])
        self.Whi = sb("Whi", [P, MID, WCOLS], F32R)
        self.Wlo = sb("Wlo", [P, MID, WCOLS], F32R)
        self.W1 = sb("W1", [64, 6, P], F32R)
        self.W7 = sb("W7", [P, 8, 4])
        self.fb = sb("fb", [P, 13])
        self.sel = sb("sel", [64, 2])
        self.iota = sb("iota", [P, 16])
        self.count_i = sb("count_i", [P, 1], U32)


def stage1_spectrum(nc, const, xs_in, pct_in, se_in, K_in, W1_in, Wm_in, others, spec, recs):
    with ExitStack() as ctx:
        def sb(name, shape, dt=F32):
            return ctx.enter_context(nc.sbuf_tensor(name, shape, dt))

        def sem(name):
            return ctx.enter_context(nc.semaphore(name))

        xg = sb("xg", [P, RING1, GM * 2, P])
        pg = sb("pg", [P, RING1, GM * 2, NLAT])
        cg = sb("cg", [P, 2, GM * 2, P])
        se = sb("se", [P, MMAX * 2])
        stage = sb("stage", [P, 2, GM, NLAT])
        rec0 = sb("rec0", [P, 8, ROW])
        Kf = sb("Kf", [P, CH, NLON])
        Wf = sb("Wf", [P, MID, WCOLS])
        W1f = sb("W1f", [64, 6, P])
        W1h = sb("W1h", [64, 6, P], F32R)
        bank = [ctx.enter_context(nc.psum_tensor(f"s1b{i}", [P, 2, NLAT], F32)) for i in range(8)]

        se_loaded = sem("se_loaded")
        loaded = [sem(f"s1_loaded{i}") for i in range(RING1)]
        scaled = sem("s1_scaled")
        summed = sem("s1_summed")
        copied = sem("s1_copied")
        stored = [sem(f"s1_stored{i}") for i in range(2)]
        const_loaded = sem("const_loaded")
        const_hi = sem("const_hi")
        const_lo = sem("const_lo")
        rec_filled = sem("rec_filled")
        rec_stored = sem("rec_stored")

        block = ctx.enter_context(nc.Block())

        @block.sync
        def _(sp):
            def load(g, b):
                sp.dma_start(xg[:, b], xs_in[:, bass.ds(g * GM * 2, GM * 2), :]).then_inc(loaded[b], 16)
                sp.dma_start(pg[:, b], pct_in[:, bass.ds(g * GM * 2, GM * 2), :]).then_inc(loaded[b], 16)

            sp.dma_start(se[:, :], se_in).then_inc(se_loaded, 16)
            for b in range(RING1):
                load(b, b)
                if b == 1:
                    for dst, src in ((Kf[:, :, :], K_in), (Wf[:, :, :], Wm_in), (W1f[:, :, :], W1_in), *others):
                        sp.dma_start(dst, src).then_inc(const_loaded, 16)
            with nc.sync.Fori(RING1, GROUPS - RING1 + 1, RING1) as g0:
                for b in range(RING1):
                    sp.wait_ge(summed, g0 + (b - RING1 + 1))
                    load(g0 + b, b)
            sp.wait_ge(summed, GROUPS - RING1 + 1)
            sp.dma_start(xg[:, 0, 0:2], xs_in[:, GROUPS * GM * 2:, :]).then_inc(loaded[0], 16)
            sp.dma_start(pg[:, 0, 0:2], pct_in[:, GROUPS * GM * 2:, :]).then_inc(loaded[0], 16)

        @block.vector
        def _(dve):
            def scale(g, b):
                wait(dve, summed, g - 1)
                nc.vector.tensor_tensor(
                    cg[:, b % 2], xg[:, b], se_view(g), ALU.mult).then_inc(scaled, 1)

            def se_view(g):
                v = se[:, bass.ds(g * GM * 2, GM * 2)]
                return v.unsqueeze(2).to_broadcast([P, GM * 2, P])

            def split_weights():
                dve.wait_ge(const_loaded, 16 * (3 + len(others)))
                dve.wait_ge(const_hi, 3)
                for lo, full, hi in ((const.Klo, Kf, const.Khi), (const.Wlo, Wf, const.Whi), (W1f, W1f, W1h)):
                    nc.vector.tensor_tensor(lo[:, :, :], full[:, :, :], hi[:, :, :].bitcast(F32),
                                            ALU.subtract).then_inc(const_lo, 1)
                dve.wait_ge(const_lo, 3)
                nc.vector.tensor_scalar(W1f[:, :, :], W1f[:, :, :], const.sel[:, 1:2], None, ALU.mult).then_inc(const_lo, 1)
                dve.wait_ge(const_lo, 4)
                nc.vector.scalar_tensor_tensor(
                    out=const.W1[:, :, :].rearrange("p a b -> p (a b)"),
                    in0=W1h[:, :, :].bitcast(F32).rearrange("p a b -> p (a b)"), scalar=const.sel[:, 0:1],
                    in1=W1f[:, :, :].rearrange("p a b -> p (a b)"), op0=ALU.mult, op1=ALU.add).then_inc(const_lo, 1)

            nc.vector.memset(rec0[:, :, 1:ROW], 0.0).then_inc(rec_filled, 1)
            nc.vector.memset(rec0[:, :, 0:1], FAR).then_inc(rec_filled, 1)
            dve.wait_ge(se_loaded, 16)
            for b in range(RING1):
                dve.wait_ge(loaded[b], 32)
                scale(b, b)
                if b == 1:
                    split_weights()
            dve.wait_ge(const_lo, 5)
            with nc.vector.Fori(RING1, GROUPS - RING1 + 1, RING1) as g0:
                for b in range(RING1):
                    dve.wait_ge(loaded[b], g0 * (32 // RING1) + 32)
                    scale(g0 + b, b)
            dve.wait_ge(loaded[0], 32 * (GROUPS // RING1 + 1))
            dve.wait_ge(summed, GROUPS - 1)
            nc.vector.tensor_tensor(
                cg[:, 0, 0:2], xg[:, 0, 0:2],
                se[:, GROUPS * GM * 2:].unsqueeze(2).to_broadcast([P, 2, P]), ALU.mult).then_inc(scaled, 1)

        @block.tensor
        def _(pe):
            def multiply(g, b):
                pe.wait_ge(scaled, g + 1)
                wait(pe, copied, (g - 1) * 4)
                for m in range(GM):
                    for h in range(2):
                        last = nc.tensor.matmul(bank[(b % 2) * 4 + m // 2][:, m % 2, :],
                                                cg[:, b % 2, m * 2 + h, :], pg[:, b, m * 2 + h, :],
                                                start=(h == 0), stop=(h == 1))
                last.then_inc(summed, 1)

            for b in range(RING1):
                multiply(b, b)
            with nc.tensor.Fori(RING1, GROUPS - RING1 + 1, RING1) as g0:
                for b in range(RING1):
                    multiply(g0 + b, b)
            pe.wait_ge(scaled, GROUPS + 1)
            pe.wait_ge(copied, (GROUPS - 1) * 4)
            for h in range(2):
                last = nc.tensor.matmul(bank[0][:, 0, :], cg[:, 0, h, :], pg[:, 0, h, :],
                                        start=(h == 0), stop=(h == 1))
            last.then_inc(summed, 1)

        @block.scalar
        def _(act):
            def copy_out(g, b):
                act.wait_ge(summed, g + 1)
                if isinstance(g, int):
                    wait(act, stored[b % 2], 32 * (g // 2))
                else:
                    act.wait_ge(stored[b % 2], g * 16 - 16 * (b % 2))
                for j in range(4):
                    nc.scalar.copy(stage[:, b % 2, 2 * j:2 * j + 2, :],
                                   bank[(b % 2) * 4 + j][:, :, :]).then_inc(copied, 1)
                act.wait_ge(copied, g * 4 + 4)
                for c in range(2):
                    act.dma_start(spec[:, bass.ds(g * GM + c * NLAT, GM), :],
                                  stage[c * NB:(c + 1) * NB, b % 2]).then_inc(stored[b % 2], 16)

            for b in range(RING1):
                copy_out(b, b)
                if b == 0:
                    act.wait_ge(const_loaded, 16 * (3 + len(others)))
                    for hi, full in ((const.Khi, Kf), (const.Whi, Wf), (W1h, W1f)):
                        nc.scalar.copy(hi[:, :, :], full[:, :, :]).then_inc(const_hi, 1)
            with nc.scalar.Fori(RING1, GROUPS - RING1 + 1, RING1) as g0:
                for b in range(RING1):
                    copy_out(g0 + b, b)
            act.wait_ge(summed, GROUPS + 1)
            act.wait_ge(stored[0], 32 * (GROUPS // 2))
            nc.scalar.copy(stage[:, 0, 0, :], bank[0][:, 0, :]).then_inc(copied, 1)
            act.wait_ge(copied, GROUPS * 4 + 1)
            act.dma_start(spec[:, NLAT, :], stage[0:NB, 0, 0, :]).then_inc(stored[0], 16)
            act.wait_ge(stored[0], 32 * (GROUPS // 2) + 16)
            act.wait_ge(stored[1], 32 * (GROUPS // 2))

        @block.gpsimd
        def _(pool):
            pool.wait_ge(rec_filled, 2)
            view = recs.rearrange("(p q r) w -> p q r w", p=P, r=8)
            for q in range(NB * NLAT // (P * 8)):
                pool.dma_start(view[:, q], rec0[:, :, :]).then_inc(rec_stored, 16)
            pool.wait_ge(rec_stored, 16 * (NB * NLAT // (P * 8)))


def stage2_blocks(nc, const, spec, recs, out):
    with ExitStack() as ctx:
        def sb(name, shape, dt=F32):
            return ctx.enter_context(nc.sbuf_tensor(name, shape, dt))

        def sem(name):
            return ctx.enter_context(nc.semaphore(name))

        dft, Khi, Klo, band, w16 = const.dft, const.Khi, const.Klo, const.band, const.w16
        tri, ident, temp, bias, rows = const.tri, const.ident, const.temp, const.bias, const.rows
        ones = sb("ones", [P, P])
        mhalf = sb("mhalf", [P, TILES])
        xt = sb("xt", [P, 4, 4, NLAT])
        od = sb("od", [P, TILES, HALF])
        eo = sb("eo", [P, TILES, 2, HALF])
        h = sb("h", [P, 4, TILES, NLON])
        xn = sb("xn", [P, 2, TILES, NLON])
        xnhi = sb("xnhi", [P, 4, TILES, NLON], F32R)
        xnlo = sb("xnlo", [P, 4, TILES, NLON], F32R)
        xThi = sb("xThi", [P, 2, CH, NLAT], F32R)
        xTlo = sb("xTlo", [P, 2, CH, NLAT], F32R)
        keyhi = sb("keyhi", [P, CH, NLAT], F32R)
        keylo = sb("keylo", [P, CH, NLAT], F32R)
        th = sb("th", [P, TILES, NLAT])
        lg = sb("lg", [P, TILES, NLAT])
        pr = sb("pr", [P, TILES, NLAT])
        pThi = sb("pThi", [P, TILES, NLAT], F32R)
        pTlo = sb("pTlo", [P, TILES, NLAT], F32R)
        h2 = sb("h2", [P, 2, TILES, NLON])
        o = sb("o", [P, 2, TILES, NLON])
        x2 = sb("x2", [P, 2, TILES, P])
        wb = sb("wb", [P, TILES, 64])
        v4 = sb("v4", [P, 2, TILES * 4])
        rec = sb("rec", [P, 4, TILES, ROW])
        bn1 = sb("bn1", [P, TILES, 6])
        bn2 = sb("bn2", [P, TILES, 6])
        mv1 = sb("mv1", [P, 4, TILES, 2])
        mv2 = sb("mv2", [P, 2, TILES, 2])
        ve = sb("ve", [P, 2, TILES])
        rstd1 = sb("rstd1", [P, 4, TILES])
        rstd2 = sb("rstd2", [P, 2, TILES])
        sc2 = sb("sc2", [P, 2, TILES])
        sh2 = sb("sh2", [P, 2, TILES])
        mx = sb("mx", [P, TILES])
        nmx = sb("nmx", [P, TILES])
        ssum = sb("ssum", [P, 2, TILES])
        rsum = sb("rsum", [P, TILES])
        above = sb("above", [P, TILES, 2])
        mask3 = sb("mask3", [P, 2, 3])
        acc3 = sb("acc3", [P, 2, 3])
        pos = sb("pos", [P, 2, 3])
        nom = sb("nom", [P, TILES])
        fidx = sb("fidx", [P, TILES])
        idx = sb("idx", [P, 4, TILES], U32)

        ps_dft = [ctx.enter_context(nc.psum_tensor(f"ps_dft{i}", [P, NLON], F32)) for i in range(2)]
        ps_kx = [ctx.enter_context(nc.psum_tensor(f"ps_kx{i}", [P, NLON], F32)) for i in range(2)]
        ps_av = [ctx.enter_context(nc.psum_tensor(f"ps_av{i}", [P, NLON], F32)) for i in range(2)]
        ps_l = ctx.enter_context(nc.psum_tensor("ps_l", [P, TILES, NLAT], F32))
        ps_pT = ctx.enter_context(nc.psum_tensor("ps_pT", [P, TILES, NLAT], F32))

        consts_set = sem("consts_set")
        x_loaded = [sem(f"x_loaded{i}") for i in range(4)]
        out_stored = [sem(f"out_stored{i}") for i in range(2)]
        pe_dft = sem("pe_dft")
        pe_xT = sem("pe_xT")
        pe_key = sem("pe_key")
        pe_logit = sem("pe_logit")
        pe_pT = sem("pe_pT")
        pe_av = sem("pe_av")
        pe_rank = sem("pe_rank")
        act_od = sem("act_od")
        act_xnhi = sem("act_xnhi")
        act_xThi = sem("act_xThi")
        act_keyhi = sem("act_keyhi")
        act_tanh = sem("act_tanh")
        act_exp = sem("act_exp")
        act_pThi = sem("act_pThi")
        act_out = sem("act_out")
        act_pos = sem("act_pos")
        dve_eo = sem("dve_eo")
        dve_h = sem("dve_h")
        dve_bn1 = sem("dve_bn1")
        dve_mv1 = sem("dve_mv1")
        dve_xn = sem("dve_xn")
        dve_xnlo = sem("dve_xnlo")
        dve_xTlo = sem("dve_xTlo")
        dve_keylo = sem("dve_keylo")
        dve_max = sem("dve_max")
        dve_pTlo = sem("dve_pTlo")
        dve_rsum = sem("dve_rsum")
        dve_h2 = sem("dve_h2")
        dve_bn2 = sem("dve_bn2")
        dve_mv2 = sem("dve_mv2")
        dve_x2 = sem("dve_x2")
        dve_wb = sem("dve_wb")
        dve_v4 = sem("dve_v4")
        pool_l = sem("pool_l")
        pool_nmx = sem("pool_nmx")
        pool_ve = sem("pool_ve")
        pool_rstd1 = sem("pool_rstd1")
        pool_rstd2 = sem("pool_rstd2")
        pool_sc2 = sem("pool_sc2")
        pool_above = sem("pool_above")
        pool_mask = sem("pool_mask")
        pool_idx = sem("pool_idx")
        pool_rec = sem("pool_rec")
        rec_sent = [sem(f"rec_sent{i}") for i in range(4)]
        cnt_stored = sem("cnt_stored")

        block = ctx.enter_context(nc.Block())

        FIRST, LAST = -2, NB + 2
        LOOP = (7, NB - 5)

        def settled(eng):
            eng.nop(nofuse=True)

        def slots(eng, slot):
            for i in range(FIRST, LOOP[0]):
                slot(i, i % 4, lambda n: 0 <= n < NB)
            with eng.Fori(LOOP[0], LOOP[1] - 3, 4) as i0:
                for u in range(4):
                    slot(i0 + u, (LOOP[0] + u) % 4, lambda n: True)
            for i in range(LOOP[1], LAST + 1):
                slot(i, i % 4, lambda n: 0 <= n < NB)

        @block.sync
        def _(sp):
            def load(n, k):
                sp.dma_start(xt[:, k].rearrange("p (h q) w -> p h (q w)", h=2),
                             spec[n].rearrange("(h p q) w -> p h (q w)", h=2, q=2)).then_inc(x_loaded[k], 16)

            for n in range(4):
                load(n, n)

            def slot(i, k, has):
                if has(i + 6):
                    sp.wait_ge(pe_dft, (i + 2) * 2 + 2)
                    load(i + 6, (k + 2) % 4)
                if has(i - 2):
                    sp.wait_ge(act_out, (i - 2) * 2 + 2)
                    sp.dma_start(out[i - 2].rearrange("(t p) w -> p t w", p=P),
                                 o[:, k % 2]).then_inc(out_stored[k % 2], 16)

            for i in range(FIRST, LOOP[0]):
                slot(i, i % 4, lambda n: 0 <= n < NB)
            with nc.sync.Fori(LOOP[0], LOOP[1] - 7, 4) as i0:
                for u in range(4):
                    slot(i0 + u, (LOOP[0] + u) % 4, lambda n: True)
            for i in range(LOOP[1] - 4, LAST + 1):
                slot(i, i % 4, lambda n: 0 <= n < NB)
            sp.wait_ge(out_stored[0], 16 * NB // 2)
            sp.wait_ge(out_stored[1], 16 * NB // 2)

        @block.tensor
        def _(pe):
            def product3(out_ap, pairs):
                n = len(pairs)
                for j, (whi, wlo, mhi, mlo) in enumerate(pairs):
                    nc.tensor.matmul(out_ap, whi, mhi, start=(j == 0), stop=False)
                    nc.tensor.matmul(out_ap, whi, mlo, start=False, stop=False)
                    last = nc.tensor.matmul(out_ap, wlo, mhi, start=False, stop=(j == n - 1))
                return last

            def keys(i, k):
                pe.wait_ge(dve_xTlo, i * 2 + 2)
                pe.wait_ge(act_xThi, i * 2 + 2)
                for b in range(2):
                    for e in (2 * b, 2 * b + 1):
                        last = product3(ps_kx[b][:, (e % 2) * NLAT:(e % 2 + 1) * NLAT],
                                        [(Khi[:, d, e * P:(e + 1) * P], Klo[:, d, e * P:(e + 1) * P],
                                          xThi[:, k % 2, d, :], xTlo[:, k % 2, d, :]) for d in range(CH)])
                    last.then_inc(pe_key, 1)

            def probs_T(n):
                pe.wait_ge(act_exp, n * 2 + 2)
                wait(pe, dve_pTlo, n)
                for t in range(TILES):
                    for s in range(TILES):
                        last = nc.tensor.transpose(ps_pT[:, s, t * P:(t + 1) * P],
                                                   pr[:, t, s * P:(s + 1) * P], ident[:, :])
                last.then_inc(pe_pT, 1)

            def inverse_dft(n, k):
                pe.wait_ge(x_loaded[k], n * 4 + (16 - 4 * k))
                for t in range(TILES):
                    wait(pe, dve_eo, (n - 1) * 4 + 2 * t + 2)
                    for src, cols, at, start, stop in ((0, RE_EVEN, 0, True, False), (2, TOP, 0, False, True),
                                                       (2, IM_EVEN, IM_EVEN[0], True, True),
                                                       (1, RE_ODD, RE_ODD[0], True, True),
                                                       (3, IM_ODD, IM_ODD[0], True, True)):
                        last = nc.tensor.matmul(ps_dft[t][:, at:at + cols[1] - cols[0]],
                                                xt[:, k, src, t * P:(t + 1) * P],
                                                dft[:, cols[0]:cols[1]], start=start, stop=stop)
                    last.then_inc(pe_dft, 1)

            def attend(n, k):
                pe.wait_ge(act_pThi, n + 1)
                pe.wait_ge(dve_pTlo, n + 1)
                pe.wait_ge(act_xnhi, n + 1)
                pe.wait_ge(dve_xnlo, n + 1)
                for t in range(TILES):
                    wait(pe, dve_h2, (n - 1) * 2 + t + 1)
                    product3(ps_av[t][:, :],
                             [(pThi[:, s, t * P:(t + 1) * P], pTlo[:, s, t * P:(t + 1) * P],
                               xnhi[:, k, s, :], xnlo[:, k, s, :]) for s in range(TILES)]).then_inc(pe_av, 1)

            def rank(n, k):
                pe.wait_ge(pool_mask, n * 4 + 4)
                pe.wait_ge(act_tanh, n + 3 if not isinstance(n, int) else min(n + 3, NB))
                nc.tensor.matmul(ps_l[:, 0, 0:3], tri[:, :], mask3[:, k % 2, :], start=True, stop=False)
                nc.tensor.matmul(ps_l[:, 0, 0:3], ones[:, :], acc3[:, k % 2, :],
                                 start=False, stop=True).then_inc(pe_rank, 1)

            def x_T(n, k):
                pe.wait_ge(dve_xn, n * 2 + 2)
                wait(pe, dve_keylo, n * 2)
                wait(pe, act_keyhi, n * 2)
                for t in range(TILES):
                    for d in range(CH):
                        last = nc.tensor.transpose(ps_kx[t][:, d * P:(d + 1) * P],
                                                   xn[:, k % 2, t, d * P:(d + 1) * P], ident[:, :])
                    last.then_inc(pe_xT, 1)

            def logits(i, k):
                pe.wait_ge(dve_keylo, i * 2 + 2)
                pe.wait_ge(act_keyhi, i * 2 + 2)
                wait(pe, act_tanh, i)
                wait(pe, act_pos, i - 2)
                for t in range(TILES):
                    last = product3(ps_l[:, t, :],
                                    [(keyhi[:, e, t * P:(t + 1) * P], keylo[:, e, t * P:(t + 1) * P],
                                      xThi[:, k % 2, e, :], xTlo[:, k % 2, e, :]) for e in range(CH)])
                last.then_inc(pe_logit, 1)

            def slot(i, k, has):
                if has(i):
                    keys(i, k)
                if has(i - 3):
                    rank(i - 3, (k + 1) % 4)
                if has(i - 1):
                    probs_T(i - 1)
                if has(i + 2):
                    inverse_dft(i + 2, (k + 2) % 4)
                if has(i + 1):
                    x_T(i + 1, (k + 1) % 4)
                if has(i - 1):
                    attend(i - 1, (k + 3) % 4)
                if has(i):
                    logits(i, k)

            pe.wait_ge(consts_set, 4)
            slots(nc.tensor, slot)

        @block.scalar
        def _(act):
            def slot(i, k, has):
                if has(i - 1):
                    act.wait_ge(pe_logit, i)
                    wait(act, pool_l, i - 1)
                    nc.scalar.activation(th[:, :, :], ps_l[:, :, :], ACT.Tanh,
                                         bias=bias[:, 0:1]).then_inc(act_tanh, 1)
                    act.wait_ge(pool_nmx, i)
                    wait(act, pe_pT, i - 1)
                    wait(act, dve_rsum, i - 3)
                    for t in range(TILES):
                        nc.scalar.activation(pr[:, t, :], lg[:, t, :], ACT.Exp, bias=nmx[:, t:t + 1],
                                             accum_out=ssum[:, (k + 1) % 2, t:t + 1]).then_inc(act_exp, 1)
                if has(i):
                    for b in range(2):
                        act.wait_ge(pe_key, i * 2 + b + 1)
                        wait(act, pe_logit, i)
                        nc.scalar.copy(keyhi[:, 2 * b:2 * b + 2, :].rearrange("p e w -> p (e w)"),
                                       ps_kx[b][:, :]).then_inc(act_keyhi, 1)
                if has(i - 3):
                    n = i - 3
                    act.wait_ge(pe_rank, n + 1)
                    wait(act, pool_idx, (n - 1) * 3)
                    nc.scalar.copy(pos[:, (k + 1) % 2, :], ps_l[:, 0, 0:3]).then_inc(act_pos, 1)
                if has(i - 1):
                    act.wait_ge(pe_pT, i)
                    wait(act, pe_av, (i - 1) * 2)
                    nc.scalar.copy(pThi[:, :, :], ps_pT[:, :, :]).then_inc(act_pThi, 1)
                if has(i + 1):
                    n = i + 1
                    act.wait_ge(dve_xn, n * 2 + 2)
                    wait(act, pe_av, (n - 3) * 2)
                    nc.scalar.copy(xnhi[:, (k + 1) % 4], xn[:, (k + 1) % 2]).then_inc(act_xnhi, 1)
                if has(i + 2):
                    n = i + 2
                    for t in range(TILES):
                        act.wait_ge(pe_dft, n * 2 + t + 1)
                        wait(act, dve_eo, (n - 1) * 4 + 2 * t + 2)
                        nc.scalar.copy(od[:, t, :], ps_dft[t][:, HALF:NLON]).then_inc(act_od, 1)
                if has(i + 1):
                    n = i + 1
                    for t in range(TILES):
                        act.wait_ge(pe_xT, n * 2 + t + 1)
                        wait(act, pe_logit, n - 1)
                        nc.scalar.copy(xThi[:, (k + 1) % 2, :, t * P:(t + 1) * P],
                                       ps_kx[t][:, :].rearrange("p (d w) -> p d w", d=CH)).then_inc(act_xThi, 1)
                if has(i - 2):
                    n = i - 2
                    act.wait_ge(pool_sc2, n * 3 + 3)
                    act.wait_ge(dve_h2, n * 2 + 2)
                    wait(act, pool_rec, (n - 1) * 4)
                    if isinstance(n, int):
                        wait(act, out_stored[k % 2], 16 * (n // 2))
                    else:
                        act.wait_ge(out_stored[k % 2], n * 8 - 8 * (k % 2))
                    for t in range(TILES):
                        nc.scalar.activation(o[:, k % 2, t], h2[:, k % 2, t], ACT.Identity,
                                             bias=sh2[:, k % 2, t:t + 1],
                                             scale=sc2[:, k % 2, t:t + 1]).then_inc(act_out, 1)

            slots(nc.scalar, slot)

        @block.vector
        def _(dve):
            def slot(i, k, has):
                if has(i - 1):
                    dve.wait_ge(pool_l, i)
                    wait(dve, pool_nmx, i - 1)
                    for t in range(TILES):
                        nc.vector.tensor_scalar(lg[:, t, :], lg[:, t, :], temp[:, 0:1], None, ALU.mult,
                                                ALU.max, accum_out=mx[:, t:t + 1]).then_inc(dve_max, 1)
                if has(i - 2):
                    n, r4, r2 = i - 2, (k + 2) % 4, k % 2
                    dve.wait_ge(act_exp, n * 2 + 2)
                    nc.vector.reciprocal(rsum[:, :], ssum[:, r2, :]).then_inc(dve_rsum, 1)
                    dve.wait_ge(dve_rsum, n + 1)
                    wait(dve, act_out, (n - 1) * 2)
                    for t in range(TILES):
                        dve.wait_ge(pe_av, n * 2 + t + 1)
                        nc.vector.scalar_tensor_tensor(out=h2[:, r2, t], in0=ps_av[t][:, :],
                                                       scalar=rsum[:, t:t + 1], in1=h[:, r4, t],
                                                       op0=ALU.mult, op1=ALU.add).then_inc(dve_h2, 1)
                if has(i + 1):
                    n, r4, r2 = i + 1, (k + 1) % 4, (k + 1) % 2
                    dve.wait_ge(pool_rstd1, n + 1)
                    wait(dve, pe_xT, (n - 1) * 2)
                    wait(dve, act_xnhi, n - 1)
                    wait(dve, dve_xnlo, n - 1)
                    for t in range(TILES):
                        nc.vector.tensor_scalar(xn[:, r2, t], h[:, r4, t], mv1[:, r4, t, 0:1],
                                                rstd1[:, r4, t:t + 1], ALU.subtract,
                                                ALU.mult).then_inc(dve_xn, 1)
                if has(i):
                    wait(dve, pe_logit, i)
                    for b in range(2):
                        dve.wait_ge(act_keyhi, i * 2 + b + 1)
                        nc.vector.tensor_tensor(
                            keylo[:, 2 * b:2 * b + 2, :].rearrange("p e w -> p (e w)"), ps_kx[b][:, :],
                            keyhi[:, 2 * b:2 * b + 2, :].bitcast(F32).rearrange("p e w -> p (e w)"),
                            ALU.subtract).then_inc(dve_keylo, 1)
                if has(i - 1):
                    dve.wait_ge(act_pThi, i)
                    wait(dve, pe_av, (i - 1) * 2)
                    nc.vector.tensor_tensor(pTlo[:, :, :], ps_pT[:, :, :], pThi[:, :, :].bitcast(F32),
                                            ALU.subtract).then_inc(dve_pTlo, 1)
                if has(i - 2):
                    n, r2 = i - 2, k % 2
                    for t in range(TILES):
                        dve.wait_ge(dve_h2, n * 2 + t + 1)
                        wait(dve, dve_mv2, (n - 1) * 2 + t + 1)
                        nc.vector.bn_stats(bn2[:, t, :], h2[:, r2, t]).then_inc(dve_bn2, 1)
                if has(i + 2):
                    n = i + 2
                    wait(dve, dve_h, (n - 1) * 3 + 3)
                    for t in range(TILES):
                        dve.wait_ge(act_od, n * 2 + t + 1)
                        for s, op in ((0, ALU.add), (1, ALU.subtract)):
                            nc.vector.tensor_tensor(eo[:, t, s, :], ps_dft[t][:, 0:HALF],
                                                    od[:, t, :], op).then_inc(dve_eo, 1)
                if has(i - 2):
                    n, r2 = i - 2, k % 2
                    wait(dve, pool_sc2, (n - 1) * 3)
                    for t in range(TILES):
                        dve.wait_ge(dve_bn2, n * 2 + t + 1)
                        settled(dve)
                        nc.vector.bn_aggr(mv2[:, r2, t, :], bn2[:, t, :]).then_inc(dve_mv2, 1)
                if has(i + 2):
                    n, r4 = i + 2, (k + 2) % 4
                    dve.wait_ge(dve_eo, n * 4 + 4)
                    hv = h[:, r4].rearrange("p t (s w) -> p t s w", s=2)
                    nc.vector.tensor_tensor(hv[:, :, :, 1:Q], eo[:, :, :, 1:Q], eo[:, :, :, Q + 1:HALF],
                                            ALU.add).then_inc(dve_h, 1)
                    nc.vector.tensor_tensor(hv[:, :, ::-1, HALF - 1:Q:-1], eo[:, :, :, 1:Q], eo[:, :, :, Q + 1:HALF],
                                            ALU.subtract).then_inc(dve_h, 1)
                    nc.vector.tensor_copy(h[:, r4].rearrange("p t (b w) -> p t b w", w=Q)[:, :, :, 0],
                                          eo[:, :, :, :].rearrange("p t s (c w) -> p t (s c) w", w=Q)[:, :, :, 0]
                                          ).then_inc(dve_h, 1)
                if has(i + 1):
                    n, r2 = i + 1, (k + 1) % 2
                    wait(dve, pe_logit, n - 1)
                    for t in range(TILES):
                        dve.wait_ge(act_xThi, n * 2 + t + 1)
                        nc.vector.tensor_tensor(xTlo[:, r2, :, t * P:(t + 1) * P],
                                                ps_kx[t][:, :].rearrange("p (d w) -> p d w", d=CH),
                                                xThi[:, r2, :, t * P:(t + 1) * P].bitcast(F32),
                                                ALU.subtract).then_inc(dve_xTlo, 1)
                if has(i + 2):
                    n, r4 = i + 2, (k + 2) % 4
                    dve.wait_ge(dve_h, n * 3 + 3)
                    for t in range(TILES):
                        wait(dve, dve_mv1, (n - 1) * 2 + t + 1)
                        nc.vector.bn_stats(bn1[:, t, :], h[:, r4, t]).then_inc(dve_bn1, 1)
                if has(i - 2):
                    n, r2 = i - 2, k % 2
                    dve.wait_ge(pool_rstd2, n + 1)
                    wait(dve, pool_rec, (n - 1) * 4)
                    wait(dve, pool_above, n - 1)
                    for t in range(TILES):
                        nc.vector.tensor_scalar(x2[:, r2, t, :], h2[:, r2, t, 0:P], mv2[:, r2, t, 0:1],
                                                rstd2[:, r2, t:t + 1], ALU.subtract,
                                                ALU.mult).then_inc(dve_x2, 1)
                if has(i + 2):
                    n, r4 = i + 2, (k + 2) % 4
                    wait(dve, pool_rstd1, n - 3)
                    for t in range(TILES):
                        dve.wait_ge(dve_bn1, n * 2 + t + 1)
                        settled(dve)
                        nc.vector.bn_aggr(mv1[:, r4, t, :], bn1[:, t, :]).then_inc(dve_mv1, 1)
                if has(i - 2):
                    n = i - 2
                    dve.wait_ge(dve_x2, n * 2 + 2)
                    wait(dve, dve_v4, n)
                    for t in range(TILES):
                        last = nc.vector.scalar_tensor_tensor(out=wb[:, t, :], in0=x2[:, k % 2, t, 64:128], scalar=0.5,
                                                              in1=w16[:, :], op0=ALU.is_gt, op1=ALU.mult)
                    last.then_inc(dve_wb, 1)
                if has(i + 1):
                    n, r4, r2 = i + 1, (k + 1) % 4, (k + 1) % 2
                    dve.wait_ge(act_xnhi, n + 1)
                    wait(dve, pe_av, (n - 3) * 2)
                    nc.vector.tensor_tensor(xnlo[:, r4], xn[:, r2], xnhi[:, r4].bitcast(F32),
                                            ALU.subtract).then_inc(dve_xnlo, 1)
                if has(i - 2):
                    dve.wait_ge(dve_wb, i - 1)
                    nc.vector.tensor_reduce(v4[:, k % 2, :], wb[:, :, :].rearrange("p t (g w) -> p (t g) w", w=16),
                                            AX_X, ALU.max).then_inc(dve_v4, 1)

            nc.vector.memset(ones[:, :], 1.0).then_inc(consts_set, 1)
            nc.vector.memset(mhalf[:, :], -0.5).then_inc(consts_set, 1)
            nc.vector.memset(mask3[:, :, :], 0.0).then_inc(consts_set, 1)
            nc.vector.memset(acc3[:, :, :], 0.0).then_inc(consts_set, 1)
            nc.vector.memset(rec[:, :, :, :], 0.0).then_inc(consts_set, 1)
            slots(nc.vector, slot)

        @block.gpsimd
        def _(pool):
            def slot(i, k, has):
                if has(i - 1):
                    pool.wait_ge(act_tanh, i)
                    wait(pool, act_exp, (i - 1) * 2)
                    nc.gpsimd.tensor_tensor(lg[:, :, :], th[:, :, :], band[:, :, :], ALU.add).then_inc(pool_l, 1)
                if has(i + 1):
                    n, r4 = i + 1, (k + 1) % 4
                    pool.wait_ge(dve_mv1, n * 2 + 2)
                    settled(pool)
                    nc.gpsimd.tensor_scalar(ve[:, 0, :], mv1[:, r4, :, 1], EPS, None, ALU.add).then_inc(pool_ve, 1)
                    pool.wait_ge(pool_ve, (max(n - 3, 0) if isinstance(n, int) else n - 3) + n + 1)
                    wait(pool, dve_xn, (n - 3) * 2)
                    nc.gpsimd.tensor_tensor(rstd1[:, r4, :], ve[:, 0, :], mhalf[:, :], ALU.pow).then_inc(pool_rstd1, 1)
                if has(i - 1):
                    pool.wait_ge(dve_max, i * 2)
                    settled(pool)
                    nc.gpsimd.tensor_scalar(nmx[:, :], mx[:, :], -1.0, None, ALU.mult).then_inc(pool_nmx, 1)
                if has(i - 3):
                    n, r2 = i - 3, (k + 1) % 2
                    pool.wait_ge(dve_x2, n * 2 + 2)
                    settled(pool)
                    nc.gpsimd.tensor_scalar(above[:, :, :], x2[:, r2, :, 0:2], 0.5, None, ALU.is_ge).then_inc(pool_above, 1)
                    pool.wait_ge(pool_above, n + 1)
                    nc.gpsimd.tensor_tensor(mask3[:, r2, 0:2], above[:, :, 0], above[:, :, 1], ALU.mult).then_inc(pool_mask, 1)
                    nc.gpsimd.tensor_copy(acc3[:, r2, 0:1], acc3[:, 1 - r2, 2:3]).then_inc(pool_mask, 1)
                    pool.wait_ge(pool_mask, n * 4 + 2)
                    nc.gpsimd.tensor_tensor(acc3[:, r2, 1:2], acc3[:, r2, 0:1], mask3[:, r2, 0:1],
                                            ALU.add).then_inc(pool_mask, 1)
                    pool.wait_ge(pool_mask, n * 4 + 3)
                    nc.gpsimd.tensor_tensor(acc3[:, r2, 2:3], acc3[:, r2, 1:2], mask3[:, r2, 1:2],
                                            ALU.add).then_inc(pool_mask, 1)
                    if not isinstance(n, int) or n + 1 < NB:
                        pool.wait_ge(pool_mask, n * 4 + 4)
                if has(i - 3):
                    n, r4, r2 = i - 3, (k + 1) % 4, (k + 1) % 2
                    if isinstance(n, int):
                        wait(pool, rec_sent[r4], 32 * (n // 4))
                    else:
                        pool.wait_ge(rec_sent[r4], n * 8 - 8 * r4)
                    pool.wait_ge(dve_v4, n + 1)
                    pool.wait_ge(act_pos, n + 1)
                    settled(pool)
                    nc.gpsimd.tensor_scalar(nom[:, :], mask3[:, r2, 0:2], -FAR, FAR, ALU.mult,
                                            ALU.add).then_inc(pool_idx, 1)
                    pool.wait_ge(pool_idx, n * 3 + 1)
                    nc.gpsimd.tensor_tensor(fidx[:, :], pos[:, r2, 0:2], nom[:, :], ALU.add).then_inc(pool_idx, 1)
                    pool.wait_ge(pool_idx, n * 3 + 2)
                    settled(pool)
                    nc.gpsimd.tensor_copy(idx[:, r4, :], fidx[:, :]).then_inc(pool_idx, 1)
                    nc.gpsimd.tensor_copy(rec[:, r4, :, 0], rows[:, :]).then_inc(pool_rec, 1)
                    nc.gpsimd.tensor_copy(rec[:, r4, :, 1:5],
                                          v4[:, r2, :].rearrange("p (t g) -> p t g", t=TILES)).then_inc(pool_rec, 1)
                    nc.gpsimd.tensor_copy(rec[:, r4, :, 5], x2[:, r2, :, 29]).then_inc(pool_rec, 1)
                    pool.wait_ge(act_out, n * 2 + 2)
                    settled(pool)
                    nc.gpsimd.tensor_copy(rec[:, r4, :, 8:ROW],
                                          o[:, r2, :, OUT_LO:OUT_LO + OUT_W]).then_inc(pool_rec, 1)
                    pool.wait_ge(pool_rec, n * 4 + 4)
                    pool.wait_ge(pool_idx, n * 3 + 3)
                    settled(pool)
                    nc.gpsimd.tensor_scalar(rows[:, :], rows[:, :], float(NLAT * 16), None, ALU.add)
                    for t in range(TILES):
                        nc.gpsimd.indirect_dma_start(
                            out=recs[:, :], out_offset=bass.IndirectOffsetOnAxis(ap=idx[:, r4, t:t + 1], axis=0),
                            in_=rec[:, r4, t, :], in_offset=None, bounds_check=NB * NLAT - 1,
                            oob_is_err=False).then_inc(rec_sent[r4], 16)
                if has(i - 2):
                    n, r2 = i - 2, k % 2
                    pool.wait_ge(dve_mv2, n * 2 + 2)
                    settled(pool)
                    nc.gpsimd.tensor_scalar(ve[:, 1, :], mv2[:, r2, :, 1], EPS, None, ALU.add).then_inc(pool_ve, 1)
                    pool.wait_ge(pool_ve, n + 1 + (min(n + 4, NB) if isinstance(n, int) else n + 4))
                    nc.gpsimd.tensor_tensor(rstd2[:, r2, :], ve[:, 1, :], mhalf[:, :], ALU.pow).then_inc(pool_rstd2, 1)
                    pool.wait_ge(pool_rstd2, n + 1)
                    wait(pool, act_out, (n - 1) * 2)
                    settled(pool)
                    nc.gpsimd.tensor_scalar(sc2[:, r2, :], rstd2[:, r2, :], 1.0, None, ALU.add).then_inc(pool_sc2, 1)
                    for t in range(TILES):
                        nc.gpsimd.tensor_scalar(sh2[:, r2, t:t + 1], mv2[:, r2, t, 0:1], rstd2[:, r2, t:t + 1], -1.0,
                                                ALU.mult, ALU.mult).then_inc(pool_sc2, 1)

            pool.wait_ge(consts_set, 5)
            slots(nc.gpsimd, slot)
            for r in range(4):
                pool.wait_ge(rec_sent[r], 32 * (NB // 4))
            nc.gpsimd.tensor_copy(const.count_i[:, :], pos[:, (NB - 1) % 2, 2:3])


def stage3_ffn(nc, const, recs, out):
    with ExitStack() as ctx:
        def sb(name, shape, dt=F32):
            return ctx.enter_context(nc.sbuf_tensor(name, shape, dt))

        def sem(name):
            return ctx.enter_context(nc.semaphore(name))

        Whi, Wlo, W1, W7, fb, ident = const.Whi, const.Wlo, const.W1, const.W7, const.fb, const.ident
        rt = sb("rt", [P, 2, TJ, ROW])
        n16 = sb("n16", [P, TJ, 4])
        oph = sb("oph", [P, TJ], F32R)
        feat = sb("feat", [P, TJ, 64])
        xin = sb("xin", [64, TJ * P], F32R)
        act_f = sb("act_f", [P, 2, 5, 512])
        act_hi = sb("act_hi", [P, 2, 5, 512], F32R)
        act_lo = sb("act_lo", [P, 2, 5, 512], F32R)
        y4 = sb("y4", [4, 512])
        res = sb("res", [P, 4, 2 * TJ])
        hot = sb("hot", [P, 2 * TJ, 16])
        oc = sb("oc", [P, TJ, OUT_W])
        dest = sb("dest", [P, TJ], U32)

        ps_main = [ctx.enter_context(nc.psum_tensor(f"ps_main{i}", [P, 512], F32)) for i in range(5)]
        ps_x = [ctx.enter_context(nc.psum_tensor(f"ps_x{i}", [P, 512], F32)) for i in range(2)]
        ps_y = ctx.enter_context(nc.psum_tensor("ps_y", [4, 512], F32))

        start = sem("ffn_start")
        rec_loaded = [sem(f"rec_loaded{i}") for i in range(2)]
        rec_used = sem("rec_used")
        oc_free = sem("oc_free")
        feat_part = sem("feat_part")
        feat_made = sem("feat_made")
        feat_T = sem("feat_T")
        xin_made = sem("xin_made")
        pe_layer = sem("pe_layer")
        act_relu = sem("act_relu")
        dve_relu = sem("dve_relu")
        dve_relo = sem("dve_relo")
        pe_y = sem("pe_y")
        act_y = sem("act_y")
        pe_yT = sem("pe_yT")
        dve_res = sem("dve_res")
        dve_hot = sem("dve_hot")
        scattered = sem("scattered")

        block = ctx.enter_context(nc.Block())
        LAYERS = MID + 1
        TOK = TJ * P
        STEPS = NB * NLAT // TOK

        def steps(eng, ahead, body):
            count = eng.value_load(const.count_i[0:1, 0:1], min_val=0, max_val=NB * NLAT)

            with eng.If(count > 0):
                ahead()
            with eng.Fori(0, STEPS, 2) as s0:
                for u in range(2):
                    s = s0 + u
                    with eng.If(count > s * TOK):
                        body(s, u, lambda: eng.If(count > (s + 1) * TOK))

        @block.sync
        def _(sp):
            def load(s, u):
                sp.dma_start(rt[:, u], recs[bass.ds(s * TOK, TOK), :]
                             .rearrange("(p j) w -> p j w", p=P)).then_inc(rec_loaded[u], 16)

            def load_in_range(s, u):
                load(nc.s_assert_within(s, 0, STEPS - 1), u)

            def body(s, u, coming):
                with coming():
                    sp.wait_ge(rec_used, s + 1)
                    sp.nop(nofuse=True)
                    load_in_range(s + 1, 1 - u)

            sp.wait_ge(start, 2)
            steps(nc.sync, lambda: load(0, 0), body)

        @block.vector
        def _(dve):
            def features(s, u):
                r = rt[:, u]
                v = r[:, :, 1:5]
                dve.wait_ge(rec_loaded[u], s * 8 + (16 - 8 * u))
                nc.vector.tensor_scalar(n16[:, :, :], v, 0.0, 16.0, ALU.is_gt, ALU.mult).then_inc(feat_part, 1)
                nc.vector.tensor_copy(oph[:, :], r[:, :, 5]).then_inc(feat_part, 1)
                dve.wait_ge(feat_part, s * 2 + 2)
                f4 = feat[:, :, :].rearrange("p j (q w) -> p j q w", q=2)
                for at in (0, 4):
                    nc.vector.tensor_tensor(f4[:, :, :, at:at + 2], n16[:, :, :].rearrange("p j (b q) -> p j q b", q=2),
                                            v.rearrange("p j (b q) -> p j q b", q=2), ALU.subtract).then_inc(feat_made, 1)
                high = oph[:, :].bitcast(F32).unsqueeze(2).to_broadcast([P, TJ, 2])
                for at in (2, 6):
                    nc.vector.tensor_copy(f4[:, :, :, at], high).then_inc(feat_made, 1)
                nc.vector.tensor_tensor(f4[:, :, :, 3], r[:, :, 5].unsqueeze(2).to_broadcast([P, TJ, 2]), high,
                                        ALU.subtract).then_inc(feat_made, 1)

            def relu(s, L):
                for g in range(5):
                    done = s * (5 * LAYERS) + (5 * L + g + 1)
                    dve.wait_ge(pe_layer, done)
                    if L < LAYERS - 1:
                        dve.wait_ge(act_relu, s * (5 * MID) + (5 * L + g + 1))
                    col = (L if g < 4 else 6 + L)
                    nc.vector.tensor_scalar(act_f[:, L % 2, g], ps_main[g][:, :], fb[:, col:col + 1], 0.0,
                                            ALU.add, ALU.max).then_inc(dve_relu, 1)
                    if L < LAYERS - 1:
                        dve.wait_ge(dve_relu, done)
                        nc.vector.tensor_tensor(act_lo[:, L % 2, g], act_f[:, L % 2, g],
                                                act_hi[:, L % 2, g].bitcast(F32), ALU.subtract).then_inc(dve_relo, 1)

            def results(s, u):
                r = rt[:, u]
                dve.wait_ge(pe_yT, s + 1)
                nc.vector.tensor_scalar(res[:, 0].rearrange("p (q a c) -> p q a c", q=2, a=2),
                                        ps_x[0][:, 0:2 * TJ].rearrange("p (c q a) -> p q a c", q=2, a=2),
                                        fb[:, 12:13], -1.0, ALU.add, ALU.max).then_inc(dve_res, 1)
                dve.wait_ge(dve_res, s * 4 + 1)
                nc.vector.tensor_scalar(res[:, 1], res[:, 0], 16.0, MAGIC, ALU.min, ALU.add).then_inc(dve_res, 1)
                dve.wait_ge(dve_res, s * 4 + 2)
                nc.vector.tensor_scalar(res[:, 2], res[:, 1], -MAGIC, 0.0, ALU.add, ALU.max).then_inc(dve_res, 1)
                dve.wait_ge(dve_res, s * 4 + 3)
                nc.vector.tensor_scalar(res[:, 3], res[:, 2], 15.0, None, ALU.min).then_inc(dve_res, 1)
                dve.wait_ge(dve_res, s * 4 + 4)
                nc.vector.tensor_tensor(hot[:, :, :], const.iota[:, :].unsqueeze(1).to_broadcast([P, 2 * TJ, 16]),
                                        res[:, 3].unsqueeze(2).to_broadcast([P, 2 * TJ, 16]), ALU.is_equal).then_inc(dve_hot, 1)
                dve.wait_ge(dve_hot, s + 1)
                dve.wait_ge(oc_free, s + 1)
                for q in range(2):
                    nc.vector.scalar_tensor_tensor(out=oc[:, :, q * 16:(q + 1) * 16], in0=hot[:, q * TJ:(q + 1) * TJ],
                                                   scalar=2.0, in1=r[:, :, 8 + q * 16:24 + q * 16],
                                                   op0=ALU.mult, op1=ALU.add)
                nc.vector.tensor_copy(dest[:, :], r[:, :, 0]).then_inc(rec_used, 1)

            def first():
                features(0, 0)
                relu(0, 0)

            def body(s, u, coming):
                relu(s, 1)
                with coming():
                    features(s + 1, 1 - u)
                for L in range(2, LAYERS):
                    relu(s, L)
                with coming():
                    relu(s + 1, 0)
                results(s, u)

            nc.vector.memset(feat[:, :, :], 0.0).then_inc(start, 1)
            nc.vector.memset(rt[:, :, :, :], 0.0).then_inc(rec_used, 1)
            nc.vector.memset(res[:, :, :], 0.0).then_inc(start, 1)
            dve.wait_ge(start, 2)
            steps(nc.vector, first, body)

        @block.scalar
        def _(act):
            def round_in(s):
                act.wait_ge(feat_T, s + 1)
                for a in range(2):
                    nc.scalar.copy(xin[:, a * 512:(a + 1) * 512], ps_x[a][0:64, :]).then_inc(xin_made, 1)

            def relu(s, L):
                for g in range(5):
                    act.wait_ge(pe_layer, s * (5 * LAYERS) + (5 * L + g + 1))
                    col = (L if g < 4 else 6 + L)
                    nc.scalar.activation(act_hi[:, L % 2, g], ps_main[g][:, :], ACT.Relu,
                                         bias=fb[:, col:col + 1]).then_inc(act_relu, 1)

            def first():
                round_in(0)
                relu(0, 0)

            def body(s, u, coming):
                for L in range(1, LAYERS - 1):
                    relu(s, L)
                with coming():
                    round_in(s + 1)
                    relu(s + 1, 0)
                act.wait_ge(pe_y, s + 1)
                nc.scalar.copy(y4[:, :], ps_y[:, :]).then_inc(act_y, 1)

            steps(nc.scalar, first, body)

        @block.tensor
        def _(pe):
            def features_T(s):
                pe.wait_ge(feat_made, s * 5 + 5)
                pe.nop(nofuse=True)
                for j in range(TJ):
                    last = nc.tensor.transpose(ps_x[j // 4][0:64, (j % 4) * P:(j % 4 + 1) * P], feat[:, j, :], ident[:, :])
                last.then_inc(feat_T, 1)

            def first_layer(s):
                pe.wait_ge(xin_made, s * 2 + 2)
                for g in range(4):
                    wait(pe, dve_relu, s * (5 * LAYERS) - 4 + g)
                    nc.tensor.matmul(ps_main[g][:, :], W1[:, g // 2, :], xin[:, (g % 2) * 512:(g % 2 + 1) * 512],
                                     start=True, stop=True).then_inc(pe_layer, 1)
                wait(pe, dve_relu, s * (5 * LAYERS))
                for g in range(4):
                    last = nc.tensor.matmul(ps_main[4][:, :], W1[:, 2 + g, :], xin[:, (g % 2) * 512:(g % 2 + 1) * 512],
                                            start=(g == 0), stop=(g == 3))
                last.then_inc(pe_layer, 1)

            def layer(s, L):
                src = (L - 1) % 2

                def ready(g):
                    pe.wait_ge(dve_relo, s * (5 * MID) + (5 * (L - 1) + g + 1))

                def product(out_ap, lo, hi, cols, g, start, stop):
                    w = L - 1
                    nc.tensor.matmul(out_ap, Whi[lo:hi, w, cols], act_hi[lo:hi, src, g], start=start, stop=False)
                    nc.tensor.matmul(out_ap, Whi[lo:hi, w, cols], act_lo[lo:hi, src, g], start=False, stop=False)
                    return nc.tensor.matmul(out_ap, Wlo[lo:hi, w, cols], act_hi[lo:hi, src, g], start=False, stop=stop)

                def main(g):
                    ready(g)
                    product(ps_main[g][:, :], 0, P, slice(0, P), g, True, False)

                def rest(g):
                    product(ps_main[g][:, :], 32 * g, 32 * g + 32, slice(P, 2 * P), 4, False, True).then_inc(pe_layer, 1)

                for g in range(4):
                    main(g)
                ready(4)
                for g in range(4):
                    rest(g)
                for g in range(4):
                    at = 2 * P + 96 - 32 * g
                    product(ps_main[4][:, :], 0, P, slice(at, at + P), g, g == 0, False)
                product(ps_main[4][:, :], 0, P, slice(2 * P + 224, 3 * P + 224), 4, False, True).then_inc(pe_layer, 1)

            def last_layer(s):
                pe.wait_ge(dve_relu, s * (5 * LAYERS) + 5 * LAYERS)
                for g in range(5):
                    last = nc.tensor.matmul(ps_y[:, :], W7[:, g, :], act_f[:, (LAYERS - 1) % 2, g],
                                            start=(g == 0), stop=(g == 4))
                last.then_inc(pe_y, 1)

            def results_T(s):
                pe.wait_ge(act_y, s + 1)
                for c in range(4):
                    last = nc.tensor.matmul(ps_x[0][:, c * 4:c * 4 + 4], y4[:, c * P:(c + 1) * P], ident[0:4, 0:4],
                                            start=True, stop=True)
                last.then_inc(pe_yT, 1)

            def first():
                features_T(0)
                first_layer(0)

            def body(s, u, coming):
                for L in range(1, LAYERS):
                    layer(s, L)
                    if L == LAYERS - 2:
                        with coming():
                            features_T(s + 1)
                with coming():
                    first_layer(s + 1)
                last_layer(s)
                results_T(s)

            steps(nc.tensor, first, body)

        @block.gpsimd
        def _(pool):
            out_rows = out.rearrange("n k (g w) -> (n k g) w", w=OUT_W)

            def body(s, u, coming):
                pool.wait_ge(rec_used, s + 2)
                pool.nop(nofuse=True)
                for j in range(TJ):
                    nc.gpsimd.indirect_dma_start(
                        out=out_rows, out_offset=bass.IndirectOffsetOnAxis(ap=dest[:, j:j + 1], axis=0),
                        in_=oc[:, j, :], in_offset=None, bounds_check=NB * NLAT * (NLON // OUT_W) - 1,
                        oob_is_err=False).then_inc(scattered, 16)
                pool.wait_ge(scattered, s * (16 * TJ) + 16 * TJ)
                pool.sem_inc(oc_free, 1)

            nc.gpsimd.memset(oc[:, :, :], 0.0).then_inc(oc_free, 1)
            steps(nc.gpsimd, lambda: pool.nop(), body)


def build(nc, xs, pct, se, K, temp, bias, W1, Wm, W7, fb, dft, band, w16, row, tri, ident, sel, iota, out):
    ctx = ExitStack()
    with ctx:
        spec = nc.dram_tensor("spec", (NB, 2 * NLAT, NLAT), F32, kind="Internal").ap()
        recs = nc.dram_tensor("recs", (NB * NLAT, ROW), F32, kind="Internal").ap()
        const = OnChip(nc, ctx)
        others = [(const.dft[:, :], dft), (const.band[:, :, :], band), (const.w16[:, :], w16), (const.tri[:, :], tri),
                  (const.ident[:, :], ident), (const.temp[:, :], temp.to_broadcast([P, 1])),
                  (const.bias[:, :], bias.to_broadcast([P, 1])), (const.rows[:, :], row), (const.W7[:, :, :], W7),
                  (const.fb[:, :], fb), (const.sel[:, :], sel), (const.iota[:, :], iota)]
        stage1_spectrum(nc, const, xs, pct, se, K, W1, Wm, others, spec, recs)
        stage2_blocks(nc, const, spec, recs, out)
        stage3_ffn(nc, const, recs, out)


def constants():
    p = np.arange(P)[:, None].astype(np.float64)
    dft = np.zeros((P, DFT_COLS))

    def angle(odd, j):
        return 2 * np.pi * np.mod((2 * p + odd) * j[None, :], NLON) / NLON

    j = np.arange(Q + 1)
    jq = np.where(j[:Q] == 0, Q, j[:Q])
    dft[:, slice(*RE_EVEN)] = np.where(p == 0, 1.0, 2.0) * np.cos(angle(0, j))
    dft[:, slice(*IM_EVEN)] = -2.0 * np.sin(angle(0, j[1:Q]))
    dft[:, slice(*RE_ODD)] = 2.0 * np.cos(angle(1, j[:Q]))
    dft[:, slice(*IM_ODD)] = -2.0 * np.sin(angle(1, jq))
    dft[0, slice(*TOP)] = np.cos(np.pi * j)
    q = np.arange(NLAT)[:, None]
    t = np.arange(NLAT)[None, :]
    inside = (q - 6 <= t) & (t < q + 6)
    band = np.where(inside, 0.0, -10000.0).reshape(TILES, P, NLAT).transpose(1, 0, 2)
    w16 = np.tile(16.0 - np.arange(16), 4)[None, :].repeat(P, 0)
    row = (np.arange(TILES)[None, :] * P + np.arange(P)[:, None]) * 16.0 + OUT_LO // OUT_W
    tri = (np.arange(P)[:, None] < np.arange(P)[None, :])
    sel = np.zeros((64, 2))
    for at in (0, 32):
        sel[at:at + 4, 0] = 1.0
        sel[at + 4:at + 7, 1] = 1.0
    iota = np.arange(16)[None, :].repeat(P, 0)
    f = lambda a: np.ascontiguousarray(a, dtype=np.float32)
    return dict(dft=f(dft), band=f(band), w16=f(w16), row=f(row), tri=f(tri), ident=f(np.eye(P)),
                sel=f(sel), iota=f(iota))


def ffn_layout(W, b):
    T = W.transpose(0, 2, 1)
    W1 = np.zeros((64, 6, P), W.dtype)
    for q in range(2):
        for r, d in enumerate((0, 1, 30, 30, 0, 1, 30)):
            W1[32 * q + r, q] = T[0, d, 0:P]
            for g in (2 * q, 2 * q + 1):
                W1[32 * q + r, 2 + g, 32 * g:32 * g + 32] = T[0, d, P:]
    Wm = np.zeros((P, MID, WCOLS), W.dtype)
    for w in range(MID):
        t = T[1 + w]
        Wm[:, w, 0:P] = t[0:P, 0:P]
        for g in range(4):
            Wm[32 * g:32 * g + 32, w, P:2 * P] = t[P:, 0:P]
            Wm[32 * g:32 * g + 32, w, 2 * P + 224 + 32 * g:2 * P + 256 + 32 * g] = t[P:, P:]
        Wm[:, w, 2 * P + 96:2 * P + 128] = t[0:P, P:]
    W7 = np.zeros((P, 8, 4), W.dtype)
    fb = np.zeros((P, 13), b.dtype)
    for g in range(4):
        W7[:, g, g] = T[6, 0:P, 2]
        W7[32 * g:32 * g + 32, 4, g] = T[6, P:, 2]
        fb[32 * g:32 * g + 32, 6:12] = b[0:6, P:].T
    fb[:, 0:6] = b[0:6, 0:P].T
    fb[:, 12] = b[6, 2]
    return dict(W1=W1, Wm=Wm, W7=W7, fb=fb)


def kernel(**inputs):
    import concourse.bacc as _bacc
    from concourse.bass_utils import run_bass_kernel_spmd as _run

    nc = _bacc.Bacc("TRN2", target_bir_lowering=False, num_devices=1)
    x = np.asarray(inputs["x"])
    xs = x.reshape(NB, 2, P, MMAX, 2).transpose(2, 3, 1, 4, 0).reshape(P, MMAX * 2, P)
    pct = np.asarray(inputs["L0_tok_pct"]).reshape(MMAX, 2, P, NLAT).transpose(2, 0, 1, 3).reshape(P, MMAX * 2, NLAT)
    se = np.asarray(inputs["L0_tok_sqrt_eig"])[0].reshape(2, P, MMAX).transpose(1, 2, 0).reshape(P, MMAX * 2)
    K = np.asarray(inputs["L0_attn_K"]).reshape(CH, P, NLON).transpose(1, 0, 2)
    arrays = dict(xs=xs, pct=pct, se=se, K=K,
                  temp=np.asarray(inputs["L0_attn_temperature"]).reshape(1, 1),
                  bias=np.asarray(inputs["L0_attn_bias"]).reshape(1, 1),
                  **ffn_layout(np.asarray(inputs["L0_ffn_W"]), np.asarray(inputs["L0_ffn_b"])), **constants())
    sent, args = {}, []
    for name, a in arrays.items():
        a = np.ascontiguousarray(a)
        sent[f"in_{name}_dram"] = a
        args.append(nc.dram_tensor(f"in_{name}_dram", a.shape, mybir.dt.from_np(a.dtype), kind="ExternalInput").ap())
    args.append(nc.dram_tensor("out_0_dram", (NB, NLAT, NLON), F32, kind="ExternalOutput").ap())
    build(nc, *args)
    r = _run(nc, [sent], core_ids=[0])
    return r.results[0]["out_0_dram"]
```
